# Optimizing a Trainium2 kernel written in Bass

```python
import numpy as np
import jax
import jax.numpy as jnp

def _softmax(x, axis=-1):
    return jax.nn.softmax(x, axis=axis)

def _gelu(x):
    return jax.nn.gelu(x, approximate=True)

def _silu(x):
    return jax.nn.silu(x)

def _sigmoid(x):
    return jax.nn.sigmoid(x)

def _layernorm(x, axis=-1, eps=1e-05):
    m = jnp.mean(x, axis=axis, keepdims=True)
    v = jnp.var(x, axis=axis, keepdims=True)
    return (x - m) / jnp.sqrt(v + eps)

def _scatter_add(tgt, idx, src, axis=0):
    return tgt.at[idx].add(src)

def _segment_sum(src, seg, n):
    return jax.ops.segment_sum(src, seg, n)
kernel_name = 'mk_decoder_preln_d2_seqx_r4_fab776'

def setup_inputs(seed: int=0):
    np.random.seed(seed)
    _w = jnp.asarray

    def _rec_inputs():
        import jax
        import jax.numpy as jnp
        _rk = jax.random.key(seed)
        x = -0.000125 + 0.9999 * jax.random.normal(jax.random.fold_in(_rk, 1), (2, 512, 512), jnp.float32)
        _lenS = 512 - jax.random.randint(jax.random.fold_in(_rk, 7), (2,), 0, max(1, 512 // 4) + 1, jnp.int32)
        _lenS2 = 1024 - jax.random.randint(jax.random.fold_in(_rk, 8), (2,), 0, max(1, 1024 // 4) + 1, jnp.int32)
        _ctx_2048P = jax.random.normal(jax.random.fold_in(_rk, 11), (2, 16, 512), jnp.float32)
        _ctx_2048c = jax.random.dirichlet(jax.random.fold_in(_rk, 511), 0.3 * jnp.ones((16,), jnp.float32), (2, 1024))
        _ctx_2048t = jnp.einsum('bsk,bkd->bsd', _ctx_2048c, _ctx_2048P)
        _ctx_2048t = _ctx_2048t * jax.lax.rsqrt(jnp.mean(jnp.square(_ctx_2048t)) + 1e-12) * 0.953939
        ctx_2048 = -0.000514642 + 1.00011 * (_ctx_2048t + 0.3 * jax.random.normal(jax.random.fold_in(_rk, 611), (2, 1024, 512), jnp.float32))
        _validS = jnp.arange(512)[None, :] < _lenS[:, None]
        _validS2 = jnp.arange(1024)[None, :] < _lenS2[:, None]
        _causal = jnp.tril(jnp.ones((512, 512), dtype=bool))
        mask_BxS2_bk0 = jnp.logical_not(jnp.broadcast_to(_validS2[:, :], (2, 1024)))
        mask_BxS2_ff1 = jnp.where(jnp.ones((2, 1024), dtype=bool), 1.0, 0.0).astype(jnp.float32)
        return (x, ctx_2048, mask_BxS2_bk0, mask_BxS2_ff1)
    x, ctx_2048, mask_BxS2_bk0, mask_BxS2_ff1 = _rec_inputs()

    def _L0_attn_setup():
        import jax, jax.numpy as jnp
        import numpy as np
        NH = 16
        key = jax.random.key(seed)
        ks = jax.random.split(key, 5)
        B, T, D = (2, 512, 512)
        scale = 0.02
        return {'x': jax.random.normal(ks[0], (B, T, D), dtype=jnp.float32), 'Wq': jax.random.normal(ks[1], (D, D), dtype=jnp.float32) * scale, 'Wk': jax.random.normal(ks[2], (D, D), dtype=jnp.float32) * scale, 'Wv': jax.random.normal(ks[3], (D, D), dtype=jnp.float32) * scale, 'Wo': jax.random.normal(ks[4], (D, D), dtype=jnp.float32) * scale}
    _L0_attn_all = _L0_attn_setup()
    _L0_attn_in = {k: v for k, v in _L0_attn_all.items() if k in ('Wq', 'Wk', 'Wv', 'Wo')}
    del _L0_attn_all

    def _L0_xattn_setup():
        import jax, jax.numpy as jnp
        import numpy as np
        key = jax.random.key(seed)
        k1, k2, k3 = jax.random.split(key, 3)
        B, S, D, M = (8, 512, 512, 128)
        hidden_states = jax.random.normal(k1, (B, S, D), dtype=jnp.float32)
        memory_tokens = jax.random.normal(k2, (B, M, D), dtype=jnp.float32)
        memory_mask = jax.random.randint(k3, (B, M), 0, 2).astype(jnp.bool_)
        return {'hidden_states': hidden_states, 'memory_tokens': memory_tokens, 'memory_mask': memory_mask}
    _L0_xattn_all = _L0_xattn_setup()
    _L0_xattn_in = {k: v for k, v in _L0_xattn_all.items() if k in ()}
    del _L0_xattn_all

    def _L0_ffn_setup():
        import jax, jax.numpy as jnp
        import numpy as np
        H = 512
        I = 352
        E = 16
        G = 4
        TOPK_GROUP = 2
        TOP_K = 6
        N_SHARED = 2
        SCALE_FACTOR = 2.5
        B, S = (2, 512)

        def _gate(hs_flat, gate_weight, bias):
            T = hs_flat.shape[0]
            logits = hs_flat @ gate_weight.T
            scores = jax.nn.sigmoid(logits)
            scores_for_choice = scores + bias[None, :]
            gs = scores_for_choice.reshape(T, G, E // G)
            group_scores = jnp.sum(jax.lax.top_k(gs, 2)[0], axis=-1)
            _, group_idx = jax.lax.top_k(group_scores, TOPK_GROUP)
            group_mask = jnp.zeros((T, G), scores.dtype).at[jnp.arange(T)[:, None], group_idx].set(1.0)
            score_mask = jnp.repeat(group_mask, E // G, axis=1)
            tmp_scores = jnp.where(score_mask > 0, scores_for_choice, 0.0)
            _, topk_idx = jax.lax.top_k(tmp_scores, TOP_K)
            topk_weight = jnp.take_along_axis(scores, topk_idx, axis=1)
            topk_weight = topk_weight / (jnp.sum(topk_weight, axis=-1, keepdims=True) + 1e-20)
            topk_weight = topk_weight * SCALE_FACTOR
            return (topk_idx, topk_weight)
        key = jax.random.key(seed)
        ks = jax.random.split(key, 8)
        scale = 0.01
        SI = I * N_SHARED
        return {'hidden_states': jax.random.normal(ks[0], (B, S, H), jnp.float32), 'gate_weight': jax.random.uniform(ks[1], (E, H), jnp.float32, -0.05, 0.05), 'e_score_correction_bias': jnp.zeros((E,), jnp.float32), 'gate_proj': jax.random.normal(ks[2], (E, I, H), jnp.float32) * scale, 'up_proj': jax.random.normal(ks[3], (E, I, H), jnp.float32) * scale, 'down_proj': jax.random.normal(ks[4], (E, H, I), jnp.float32) * scale, 'shared_gate_w': jax.random.normal(ks[5], (SI, H), jnp.float32) * scale, 'shared_up_w': jax.random.normal(ks[6], (SI, H), jnp.float32) * scale, 'shared_down_w': jax.random.normal(ks[7], (H, SI), jnp.float32) * scale}
    _L0_ffn_all = _L0_ffn_setup()
    _L0_ffn_in = {k: v for k, v in _L0_ffn_all.items() if k in ('gate_weight', 'e_score_correction_bias', 'gate_proj', 'up_proj', 'down_proj', 'shared_gate_w', 'shared_up_w', 'shared_down_w')}
    del _L0_ffn_all

    def _L1_attn_setup():
        import jax, jax.numpy as jnp
        import numpy as np
        DIM_MODEL = 512
        DQK = 64
        DV = 64
        NUM_HEADS = 32
        NUM_GROUPS = 8
        H_PER_G = NUM_HEADS // NUM_GROUPS
        ROPE_THETA = 10000.0
        RMS_EPS = 1e-06

        def _rope(x):
            d = x.shape[-1]
            s = x.shape[-2]
            inv_freq = 1.0 / ROPE_THETA ** (jnp.arange(0, d, 2, dtype=jnp.float32) / d)
            ang = jnp.arange(s, dtype=jnp.float32)[:, None] * inv_freq[None, :]
            cos, sin = (jnp.cos(ang), jnp.sin(ang))
            x1, x2 = (x[..., :d // 2], x[..., d // 2:])
            return jnp.concatenate([x1 * cos - x2 * sin, x2 * cos + x1 * sin], axis=-1)
        key = jax.random.key(seed)
        k1, k2, k3 = jax.random.split(key, 3)
        b, s = (2, 512)
        concat = NUM_HEADS * DQK + NUM_GROUPS * (DQK + DV)
        x = jax.random.normal(k1, (b, s, DIM_MODEL), dtype=jnp.float32)
        w_in = jax.random.normal(k2, (concat, DIM_MODEL), dtype=jnp.float32) * DIM_MODEL ** (-0.5)
        w_out = jax.random.normal(k3, (DIM_MODEL, NUM_HEADS * DV), dtype=jnp.float32) * (NUM_HEADS * DV) ** (-0.5)
        rms_w = jnp.ones((DIM_MODEL,), dtype=jnp.float32)
        return {'x': x, 'w_in': w_in, 'w_out': w_out, 'rms_w': rms_w}
    _L1_attn_all = _L1_attn_setup()
    _L1_attn_in = {k: v for k, v in _L1_attn_all.items() if k in ('w_in', 'w_out', 'rms_w')}
    del _L1_attn_all

    def _L1_xattn_setup():
        import jax, jax.numpy as jnp
        import numpy as np
        H = 512
        NH = 16
        HD = H // NH
        FD = 64
        key = jax.random.key(seed)
        ks = jax.random.split(key, 12)
        B, S = (4, 1024)
        s = 1.0 / np.sqrt(H)
        sf = 1.0 / np.sqrt(HD)
        return {'query': jax.random.normal(ks[0], (B, S, H), jnp.float32), 'key': jax.random.normal(ks[1], (B, S, H), jnp.float32), 'value': jax.random.normal(ks[2], (B, S, H), jnp.float32), 'attention_mask': jnp.ones((B, S), jnp.float32), 'Wq': jax.random.normal(ks[3], (H, H), jnp.float32) * s, 'bq': jnp.zeros((H,), jnp.float32), 'Wk': jax.random.normal(ks[4], (H, H), jnp.float32) * s, 'bk': jnp.zeros((H,), jnp.float32), 'Wv': jax.random.normal(ks[5], (H, H), jnp.float32) * s, 'bv': jnp.zeros((H,), jnp.float32), 'Wqf': jax.random.normal(ks[6], (FD, HD), jnp.float32) * sf, 'Wkf': jax.random.normal(ks[7], (FD, HD), jnp.float32) * sf, 'Wo': jax.random.normal(ks[8], (H, H), jnp.float32) * s, 'bo': jnp.zeros((H,), jnp.float32)}
    _L1_xattn_all = _L1_xattn_setup()
    _L1_xattn_in = {k: v for k, v in _L1_xattn_all.items() if k in ('Wq', 'bq', 'Wk', 'bk', 'Wv', 'bv', 'Wqf', 'Wkf', 'Wo', 'bo')}
    del _L1_xattn_all

    def _L1_ffn_setup():
        import jax, jax.numpy as jnp
        import numpy as np
        B, S, H = (4, 1024, 512)
        I = 352
        E = 8
        K = 2
        INIT = 0.02
        key = jax.random.key(seed)
        k0, k1, k2, k3, k4, k5 = jax.random.split(key, 6)
        return {'x': jax.random.normal(k0, (B, S, H), dtype=jnp.float32), 'w_shared1': jax.random.normal(k1, (H, I), dtype=jnp.float32) * INIT, 'w_shared2': jax.random.normal(k2, (I, H), dtype=jnp.float32) * INIT, 'w1': jax.random.normal(k3, (E, H, I), dtype=jnp.float32) * INIT, 'w2': jax.random.normal(k4, (E, I, H), dtype=jnp.float32) * INIT, 'w_router': jax.random.normal(k5, (H, E), dtype=jnp.float32) * INIT}
    _L1_ffn_all = _L1_ffn_setup()
    _L1_ffn_in = {k: v for k, v in _L1_ffn_all.items() if k in ('w_shared1', 'w_shared2', 'w1', 'w2', 'w_router')}
    del _L1_ffn_all
    return {'x': x, 'ctx_2048': ctx_2048, 'mask_BxS2_bk0': mask_BxS2_bk0, 'mask_BxS2_ff1': mask_BxS2_ff1, 'L0_attn_Wq': _L0_attn_in['Wq'], 'L0_attn_Wk': _L0_attn_in['Wk'], 'L0_attn_Wv': _L0_attn_in['Wv'], 'L0_attn_Wo': _L0_attn_in['Wo'], 'L0_ffn_gate_weight': _L0_ffn_in['gate_weight'], 'L0_ffn_e_score_correction_bias': _L0_ffn_in['e_score_correction_bias'], 'L0_ffn_gate_proj': _L0_ffn_in['gate_proj'], 'L0_ffn_up_proj': _L0_ffn_in['up_proj'], 'L0_ffn_down_proj': _L0_ffn_in['down_proj'], 'L0_ffn_shared_gate_w': _L0_ffn_in['shared_gate_w'], 'L0_ffn_shared_up_w': _L0_ffn_in['shared_up_w'], 'L0_ffn_shared_down_w': _L0_ffn_in['shared_down_w'], 'L1_attn_w_in': _L1_attn_in['w_in'], 'L1_attn_w_out': _L1_attn_in['w_out'], 'L1_attn_rms_w': _L1_attn_in['rms_w'], 'L1_xattn_Wq': _L1_xattn_in['Wq'], 'L1_xattn_bq': _L1_xattn_in['bq'], 'L1_xattn_Wk': _L1_xattn_in['Wk'], 'L1_xattn_bk': _L1_xattn_in['bk'], 'L1_xattn_Wv': _L1_xattn_in['Wv'], 'L1_xattn_bv': _L1_xattn_in['bv'], 'L1_xattn_Wqf': _L1_xattn_in['Wqf'], 'L1_xattn_Wkf': _L1_xattn_in['Wkf'], 'L1_xattn_Wo': _L1_xattn_in['Wo'], 'L1_xattn_bo': _L1_xattn_in['bo'], 'L1_ffn_w_shared1': _L1_ffn_in['w_shared1'], 'L1_ffn_w_shared2': _L1_ffn_in['w_shared2'], 'L1_ffn_w1': _L1_ffn_in['w1'], 'L1_ffn_w2': _L1_ffn_in['w2'], 'L1_ffn_w_router': _L1_ffn_in['w_router']}

def reference(x, ctx_2048, mask_BxS2_bk0, mask_BxS2_ff1, L0_attn_Wq, L0_attn_Wk, L0_attn_Wv, L0_attn_Wo, L0_ffn_gate_weight, L0_ffn_e_score_correction_bias, L0_ffn_gate_proj, L0_ffn_up_proj, L0_ffn_down_proj, L0_ffn_shared_gate_w, L0_ffn_shared_up_w, L0_ffn_shared_down_w, L1_attn_w_in, L1_attn_w_out, L1_attn_rms_w, L1_xattn_Wq, L1_xattn_bq, L1_xattn_Wk, L1_xattn_bk, L1_xattn_Wv, L1_xattn_bv, L1_xattn_Wqf, L1_xattn_Wkf, L1_xattn_Wo, L1_xattn_bo, L1_ffn_w_shared1, L1_ffn_w_shared2, L1_ffn_w1, L1_ffn_w2, L1_ffn_w_router):
    import jax
    import jax.numpy as jnp

    def _L0_attn_ref(x, Wq, Wk, Wv, Wo):
        import jax, jax.numpy as jnp
        import numpy as np
        NH = 16
        B, T, D = x.shape
        hd = D // NH
        q = (x @ Wq.T).reshape(B, T, NH, hd).transpose(0, 2, 1, 3)
        k = (x @ Wk.T).reshape(B, T, NH, hd).transpose(0, 2, 1, 3)
        v = (x @ Wv.T).reshape(B, T, NH, hd).transpose(0, 2, 1, 3)
        att = jnp.einsum('bhtd,bhsd->bhts', q, k) / jnp.sqrt(jnp.asarray(hd, x.dtype))
        neg = jnp.finfo(att.dtype).min
        mask = jnp.triu(jnp.full((T, T), neg, dtype=att.dtype), k=1)
        att = att + mask
        w = jax.nn.softmax(att, axis=-1)
        z = jnp.einsum('bhts,bhsd->bhtd', w, v)
        z = z.transpose(0, 2, 1, 3).reshape(B, T, D)
        return z @ Wo.T

    def _L0_xattn_ref(hidden_states, memory_tokens, memory_mask):
        import jax, jax.numpy as jnp
        import numpy as np
        B, S, D = hidden_states.shape
        scale = 1.0 / jnp.sqrt(jnp.asarray(D, hidden_states.dtype))
        scores = jnp.einsum('bsd,bmd->bsm', hidden_states, memory_tokens) * scale
        neg_inf = jnp.asarray(-1e+30, scores.dtype)
        scores = jnp.where(memory_mask[:, None, :], scores, neg_inf)
        attn = jax.nn.softmax(scores, axis=-1)
        readout = jnp.einsum('bsm,bmd->bsd', attn, memory_tokens)
        valid_b = jnp.any(memory_mask, axis=-1)
        out = jnp.where(valid_b[:, None, None], readout, jnp.zeros_like(readout))
        return out

    def _L0_ffn_ref(hidden_states, gate_weight, e_score_correction_bias, gate_proj, up_proj, down_proj, shared_gate_w, shared_up_w, shared_down_w):
        import jax, jax.numpy as jnp
        import numpy as np
        H = 512
        I = 352
        E = 16
        G = 4
        TOPK_GROUP = 2
        TOP_K = 6
        N_SHARED = 2
        SCALE_FACTOR = 2.5
        B, S = (2, 512)

        def _gate(hs_flat, gate_weight, bias):
            T = hs_flat.shape[0]
            logits = hs_flat @ gate_weight.T
            scores = jax.nn.sigmoid(logits)
            scores_for_choice = scores + bias[None, :]
            gs = scores_for_choice.reshape(T, G, E // G)
            group_scores = jnp.sum(jax.lax.top_k(gs, 2)[0], axis=-1)
            _, group_idx = jax.lax.top_k(group_scores, TOPK_GROUP)
            group_mask = jnp.zeros((T, G), scores.dtype).at[jnp.arange(T)[:, None], group_idx].set(1.0)
            score_mask = jnp.repeat(group_mask, E // G, axis=1)
            tmp_scores = jnp.where(score_mask > 0, scores_for_choice, 0.0)
            _, topk_idx = jax.lax.top_k(tmp_scores, TOP_K)
            topk_weight = jnp.take_along_axis(scores, topk_idx, axis=1)
            topk_weight = topk_weight / (jnp.sum(topk_weight, axis=-1, keepdims=True) + 1e-20)
            topk_weight = topk_weight * SCALE_FACTOR
            return (topk_idx, topk_weight)
        b, s, h = hidden_states.shape
        hs = hidden_states.reshape(-1, h)
        T = hs.shape[0]
        topk_idx, topk_weight = _gate(hs, gate_weight, e_score_correction_bias)
        comb = jnp.zeros((T, E), hs.dtype).at[jnp.arange(T)[:, None], topk_idx].add(topk_weight)
        out = jnp.zeros_like(hs)
        for e in range(E):
            g = hs @ gate_proj[e].T
            u = hs @ up_proj[e].T
            inter = jax.nn.silu(g) * u
            out = out + comb[:, e:e + 1] * (inter @ down_proj[e].T)
        y = out.reshape(b, s, h)
        sg = hidden_states @ shared_gate_w.T
        su = hidden_states @ shared_up_w.T
        shared_out = jax.nn.silu(sg) * su @ shared_down_w.T
        return y + shared_out

    def _L1_attn_ref(x, w_in, w_out, rms_w):
        import jax, jax.numpy as jnp
        import numpy as np
        DIM_MODEL = 512
        DQK = 64
        DV = 64
        NUM_HEADS = 32
        NUM_GROUPS = 8
        H_PER_G = NUM_HEADS // NUM_GROUPS
        ROPE_THETA = 10000.0
        RMS_EPS = 1e-06

        def _rope(x):
            d = x.shape[-1]
            s = x.shape[-2]
            inv_freq = 1.0 / ROPE_THETA ** (jnp.arange(0, d, 2, dtype=jnp.float32) / d)
            ang = jnp.arange(s, dtype=jnp.float32)[:, None] * inv_freq[None, :]
            cos, sin = (jnp.cos(ang), jnp.sin(ang))
            x1, x2 = (x[..., :d // 2], x[..., d // 2:])
            return jnp.concatenate([x1 * cos - x2 * sin, x2 * cos + x1 * sin], axis=-1)
        b, s, _ = x.shape
        y = x * jax.lax.rsqrt(jnp.mean(x * x, axis=-1, keepdims=True) + RMS_EPS) * rms_w
        y = jnp.einsum('bsm,cm->bsc', y, w_in)
        cq = NUM_HEADS * DQK
        ck = NUM_GROUPS * DQK
        q, k, v = (y[..., :cq], y[..., cq:cq + ck], y[..., cq + ck:])
        q = q.reshape(b, s, NUM_GROUPS, H_PER_G, DQK).transpose(0, 2, 3, 1, 4)
        k = k.reshape(b, s, NUM_GROUPS, DQK).transpose(0, 2, 1, 3)[:, :, None]
        v = v.reshape(b, s, NUM_GROUPS, DV).transpose(0, 2, 1, 3)[:, :, None]
        q = _rope(q)
        k = _rope(k)
        qk = jnp.einsum('bghsd,bgxpd->bghsp', q, k) * DQK ** (-0.5)
        causal = jnp.tril(jnp.ones((s, s), dtype=bool))
        qk = jnp.where(causal, qk, -jnp.inf)
        attn = jax.nn.softmax(qk, axis=-1)
        o = jnp.einsum('bghsp,bgxpd->bghsd', attn, v)
        o = o.transpose(0, 3, 1, 2, 4).reshape(b, s, NUM_HEADS * DV)
        y = jnp.einsum('bsc,mc->bsm', o, w_out)
        return x + y

    def _L1_xattn_ref(query, key, value, attention_mask, Wq, bq, Wk, bk, Wv, bv, Wqf, Wkf, Wo, bo):
        import jax, jax.numpy as jnp
        import numpy as np
        H = 512
        NH = 16
        HD = H // NH
        FD = 64
        B, Sq, _ = query.shape
        Sk = key.shape[1]

        def heads(x, W, b, S):
            return (x @ W.T + b).reshape(B, S, NH, HD).transpose(0, 2, 1, 3)
        q = heads(query, Wq, bq, Sq)
        k = heads(key, Wk, bk, Sk)
        v = heads(value, Wv, bv, Sk)
        q_prime = jax.nn.relu(jnp.einsum('bhnd,fd->bhnf', q, Wqf))
        k_prime = jax.nn.relu(jnp.einsum('bhnd,fd->bhnf', k, Wkf))
        k_prime = k_prime * attention_mask[:, None, :, None]
        kv = jnp.einsum('bhnf,bhne->bhfe', k_prime, v)
        qkv = jnp.einsum('bhmf,bhfe->bhme', q_prime, kv)
        k_sum = jnp.sum(k_prime, axis=2)
        qk_sum = jnp.einsum('bhmf,bhf->bhm', q_prime, k_sum)[..., None]
        out = qkv / (qk_sum + 1e-08)
        out = out.transpose(0, 2, 1, 3).reshape(B, Sq, H)
        return out @ Wo.T + bo

    def _L1_ffn_ref(x, w_shared1, w_shared2, w1, w2, w_router):
        import jax, jax.numpy as jnp
        import numpy as np
        B, S, H = (4, 1024, 512)
        I = 352
        E = 8
        K = 2
        INIT = 0.02
        bs, seq_len, hidden = x.shape
        xf = x.reshape(-1, hidden)
        T = xf.shape[0]
        shared = jax.nn.silu(xf @ w_shared1) @ w_shared2
        router_logits = xf @ w_router
        routing_probs = jax.nn.softmax(router_logits, axis=-1)
        top_k_probs, top_k_idx = jax.lax.top_k(routing_probs, K)
        top_k_probs = top_k_probs / jnp.sum(top_k_probs, axis=-1, keepdims=True)
        comb = jnp.zeros((T, E), dtype=xf.dtype).at[jnp.arange(T)[:, None], top_k_idx].add(top_k_probs)
        routed = jnp.zeros_like(xf)
        for e in range(E):
            expert_out = jax.nn.silu(xf @ w1[e]) @ w2[e]
            routed = routed + comb[:, e:e + 1] * expert_out
        final = (shared + routed).reshape(bs, seq_len, hidden)
        return final
    x = x + _L0_attn_ref(_layernorm(x, axis=-1), L0_attn_Wq, L0_attn_Wk, L0_attn_Wv, L0_attn_Wo)
    x = x + _L0_xattn_ref(_layernorm(x, axis=-1), ctx_2048, mask_BxS2_bk0)
    x = x + _L0_ffn_ref(_layernorm(x, axis=-1), L0_ffn_gate_weight, L0_ffn_e_score_correction_bias, L0_ffn_gate_proj, L0_ffn_up_proj, L0_ffn_down_proj, L0_ffn_shared_gate_w, L0_ffn_shared_up_w, L0_ffn_shared_down_w)
    x = x + _L1_attn_ref(_layernorm(x, axis=-1), L1_attn_w_in, L1_attn_w_out, L1_attn_rms_w)
    x = x + _L1_xattn_ref(_layernorm(x, axis=-1), ctx_2048, ctx_2048, mask_BxS2_ff1, L1_xattn_Wq, L1_xattn_bq, L1_xattn_Wk, L1_xattn_bk, L1_xattn_Wv, L1_xattn_bv, L1_xattn_Wqf, L1_xattn_Wkf, L1_xattn_Wo, L1_xattn_bo)
    x = x + _L1_ffn_ref(_layernorm(x, axis=-1), L1_ffn_w_shared1, L1_ffn_w_shared2, L1_ffn_w1, L1_ffn_w2, L1_ffn_w_router)
    return x

_drawn_inputs = setup_inputs


def setup_inputs(seed=0):
    import zlib

    import numpy as np

    out = dict(_drawn_inputs(seed))
    spreads = {'L0_ffn_e_score_correction_bias': (0.0, 0.8),
     'L1_attn_rms_w': (1.0, 0.6),
     'L1_xattn_bq': (0.0, 2.0),
     'L1_xattn_bk': (0.0, 2.0),
     'L1_xattn_bv': (0.0, 0.513),
     'L1_xattn_bo': (0.0, 0.572)}
    factors = {'L0_attn_Wq': 8.0,
     'L0_attn_Wk': 8.0,
     'L0_ffn_gate_weight': 8.0,
     'L0_ffn_gate_proj': 8.0,
     'L0_ffn_up_proj': 8.0,
     'L0_ffn_down_proj': 8.0,
     'L0_ffn_shared_gate_w': 8.0,
     'L0_ffn_shared_up_w': 8.0,
     'L0_ffn_shared_down_w': 8.0,
     'L1_xattn_Wq': 22.864,
     'L1_xattn_Wqf': 21.888,
     'L1_xattn_Wk': 8.0,
     'L1_xattn_Wkf': 8.0,
     'L1_ffn_w_shared1': 4.565,
     'L1_ffn_w_shared2': 4.459,
     'L1_ffn_w1': 6.345,
     'L1_ffn_w2': 6.22,
     'L1_ffn_w_router': 7.111}
    for name, (base, spread) in spreads.items():
        noise = np.random.default_rng([zlib.crc32(name.encode()), seed]).standard_normal(out[name].shape)
        drawn = base * np.exp(spread * noise) if base else spread * noise
        out[name] = jnp.asarray(drawn.astype(out[name].dtype))
    for name, factor in factors.items():
        out[name] = (out[name] * factor).astype(out[name].dtype)
    return out
```

```python
from contextlib import ExitStack

import concourse.bass as bass
from concourse import mybir

F32 = mybir.dt.float32
F32R = mybir.dt.float32r
BF16 = mybir.dt.bfloat16
U8 = mybir.dt.uint8
ALU = mybir.AluOpType
ACT = mybir.ActivationFunctionType
AX = mybir.AxisListType

P = 128
B, T, D = 2, 512, 512
NTOK = B * T
NT = NTOK // P
TT = T // P
KD = D // P
SC = 1024
CT = SC // P
INNER = 352
ITILES = [(0, 128), (128, 128), (256, 96)]
LN_EPS, RMS_EPS = 1e-5, 1e-6
MASKED = -1e30
SEM_START = 16384


class Mark:

    def __init__(self, sem, value, loop, back=0):
        self.sem, self.value, self.loop, self.back = sem, value, loop, back


class Loop:
    def __init__(self, n, start):
        self.n, self.start, self.per, self.index, self.over = n, start, {}, None, False


class Queue:

    ENGINES = ("pe", "act", "dve", "pool")

    def __init__(self, nc, sems):
        self.nc, self.sems = nc, sems
        self.engines = {"pe": nc.tensor, "act": nc.scalar, "dve": nc.vector, "pool": nc.gpsimd,
                        "sp": nc.sync}
        self.count = {s: 0 for s in sems}
        self.notes = {}
        self.loop_ = None
        self.dry = False
        self.seen = {e: {} for e in self.engines}
        for s in self.ENGINES:
            nc.sync.sem_inc(sems[s], SEM_START)
            self.count[s] = SEM_START

    def note(self, key, *marks):
        self.notes[key] = tuple(marks)

    def at(self, key):
        return self.notes.get(key, ())

    def _value(self, m):
        if m.loop is None:
            return m.value, None
        lp = m.loop
        if lp.over or m.back and lp is not self.loop_:
            return lp.start[m.sem] + (lp.n - 1) * lp.per.get(m.sem, 0) + m.value, None
        return lp.start[m.sem] + m.value - m.back * lp.per.get(m.sem, 0), lp

    def wait(self, eng, *marks):
        if self.dry:
            return
        most = {}
        for m in marks:
            v, lp = self._value(m)
            key = (m.sem, lp)
            most[key] = max(most.get(key, 0), v)
        for (s, lp), v in most.items():
            if self.seen[eng].get((s, lp), -1) >= v:
                continue
            self.seen[eng][(s, lp)] = v
            per = lp.per.get(s, 0) if lp else 0
            assert v > 0, (s, v)
            self.engines[eng].wait_ge(self.sems[s], lp.index * per + v if per else v)
            if per and eng in ("sp", "pool"):
                self.engines[eng].sem_inc(self.sems["passed"], 1)

    def op(self, eng, make, *waits, sem=None, by=1):
        sem = sem or eng
        if not self.dry:
            self.wait(eng, *waits)
            make(self.engines[eng]).then_inc(self.sems[sem], by)
        self.count[sem] += by
        base = self.loop_.start[sem] if self.loop_ else 0
        return Mark(sem, self.count[sem] - base, self.loop_)

    def quiet(self, eng, make, *waits):
        if not self.dry:
            self.wait(eng, *waits)
            make(self.engines[eng])

    def load(self, sem, make, *waits):
        return self.op("sp", make, *waits, sem=sem, by=16)

    def loop(self, n, body):
        lp = Loop(n, dict(self.count))
        before = dict(self.notes)
        self.loop_, self.dry = lp, True
        body(0)
        lp.per = {s: self.count[s] - lp.start[s] for s in self.count}
        ended = self.notes
        self.count = dict(lp.start)
        self.dry = False
        self.notes = dict(before)
        for k, marks in ended.items():
            back = tuple(Mark(m.sem, m.value, lp, 1) for m in marks if m.loop is lp)
            if back:
                self.notes[k] = before.get(k, ()) + back
        with self.nc.Fori(0, n) as i:
            lp.index = i
            body(i)
        assert all(self.count[s] - lp.start[s] == lp.per[s] for s in self.count)
        lp.over, self.loop_ = True, None
        self.count = {s: lp.start[s] + n * lp.per[s] for s in self.count}
        for seen in self.seen.values():
            for s, of in list(seen):
                if of is lp:
                    del seen[(s, of)]

    def fence(self):
        self.wait("sp", *[Mark(s, v, None) for s, v in self.count.items() if v and s != "fence"])
        told = self.op("sp", lambda e: e.nop(), sem="fence")
        for e in self.engines:
            if e != "sp":
                self.wait(e, told)
        self.notes = {}


def program(nc, t):
    ctx = ExitStack()
    with ctx:
        sems = {s: ctx.enter_context(nc.semaphore(f"s_{s}")) for s in
                ("pe", "act", "dve", "pool", "x", "small", "w", "w2", "ctx", "out", "turn0", "turn1", "fence", "passed")}
        q = Queue(nc, sems)
        bank = [ctx.enter_context(nc.psum_tensor(f"bank{i}", [P, 512], F32)) for i in range(8)]

        def sb(name, shape, dt=F32, scope=ctx):
            return scope.enter_context(nc.sbuf_tensor(name, [P] + list(shape), dt))

        X = sb("X", [NT, D])
        YH, YL = sb("YH", [KD, NTOK], F32R), sb("YL", [KD, NTOK], F32R)
        ident = sb("ident", [P])
        identb = sb("identb", [P], BF16)
        causal = sb("causal", [P], BF16)
        k = dict(q=q, bank=bank, sb=sb, X=X, YH=YH, YL=YL, ident=ident, identb=identb,
                 causal=causal, nc=nc)

        x_in = q.load("x", lambda e: e.dma_start(
            X[:, :, :], t["x"].rearrange("b (t p) d -> p (b t) d", p=P)))
        q.note("x", x_in)
        zero = q.op("pool", lambda e: e.memset(ident[:, :], 0.0))
        zero2 = q.op("pool", lambda e: e.memset(causal[:, :], 0.0))
        m1 = q.op("pool", lambda e: e.affine_select(
            out=ident[:, :], in_=ident[:, :], compare_op=ALU.not_equal, fill=1.0, base=0,
            pattern=[[-1, P]], channel_multiplier=1), zero)
        m2 = q.op("pool", lambda e: e.affine_select(
            out=causal[:, :], in_=causal[:, :], compare_op=ALU.is_ge, fill=MASKED, base=0,
            pattern=[[-1, P]], channel_multiplier=1), zero2)
        m3 = q.op("dve", lambda e: e.tensor_copy(identb[:, :], ident[:, :]), m1)
        q.wait("pe", m1, m2, m3)

        attention(k, "a0", t["a0_qkv"], t["a0_wo"], heads=4, qtiles=1, hd=32)
        memory_attention(k, t["ctxT"], t["ctx"], t["mem_mask"])
        norm_all(k, "n2")
        experts(k, "f0", t["f0_up"], t["f0_down"], routed=16, shared=2, gated=True,
                router=t["f0_router"], bias=t["f0_bias"])
        attention(k, "a1", t["a1_qkv"], t["a1_wo"], heads=2, qtiles=4, hd=64, rotary=t["rotary"],
                  rms=t["rms_w"])
        linear_attention(k, t)
        norm_all(k, "n5")
        experts(k, "f1", t["f1_up"], t["f1_down"], routed=8, shared=1, gated=False,
                router=t["f1_router"], bias=None)
        end = q.load("out", lambda e: e.dma_start(
            t["out"].rearrange("b (t p) d -> p (b t) d", p=P), X[:, :, :]), *q.at("x"))
        q.wait("sp", end)
        q.fence()


def split(q, eng, hi, lo, src, *waits, scale=None, bias=None):
    hi32 = hi.bitcast(F32)
    if bias is not None:
        m = q.op("act", lambda e: e.activation(hi, src, ACT.Identity, bias=bias), *waits)
        return q.op(eng, lambda e: e.scalar_tensor_tensor(
            out=lo, in0=src, scalar=bias, in1=hi32, op0=ALU.add, op1=ALU.subtract), m)
    if scale is not None:
        m = q.op("act", lambda e: e.activation(hi, src, ACT.Copy, scale=scale), *waits)
        return q.op(eng, lambda e: e.scalar_tensor_tensor(
            out=lo, in0=src, scalar=scale, in1=hi32, op0=ALU.mult, op1=ALU.subtract), m)
    m = q.op("act", lambda e: e.activation(hi, src, ACT.Copy), *waits)
    return q.op(eng, lambda e: e.tensor_tensor(lo, src, hi32, ALU.subtract), m)


def splits(q, eng, parts, *waits, scale=1.0):
    for hi, _, src in parts:
        m = q.op("act", lambda e: e.activation(hi, src, ACT.Copy, scale=scale), *waits)
    for hi, lo, src in parts:
        last = q.op(eng, lambda e: e.scalar_tensor_tensor(
            out=lo, in0=src, scalar=scale, in1=hi.bitcast(F32), op0=ALU.mult, op1=ALU.subtract), m)
    return last


def product(q, out, lhs, rhs, *waits, first=True, last=True, check=True):
    n = len(lhs)
    m = None
    for i, ((lh, ll), (rh, rl)) in enumerate(zip(lhs, rhs)):
        for j, (a, b) in enumerate(((lh, rh), (lh, rl), (ll, rh))):
            make = lambda e: e.matmul(out, a, b, start=first and i == 0 and j == 0,
                                      stop=last and i == n - 1 and j == 2,
                                      skip_group_check=not check)
            if i == n - 1 and j == 2:
                m = q.op("pe", make, *waits)
            else:
                q.quiet("pe", make, *waits)
            waits = ()
    return m


class NormBuffers:

    def __init__(self, k, scope, name, n, y=None, rms=False):
        sb = lambda nm, shape: k["sb"](f"{name}_{nm}", shape, F32, scope)
        self.stats, self.moments, self.var = sb("stats", [n, 6]), sb("moments", [n, 2]), sb("var", [n])
        self.root, self.inv, self.u = sb("root", [n]), sb("inv", [n]), sb("u", [n])
        self.y = [sb(f"y{i}", [D])[:, :] for i in range(min(n, 4))] if y is None else y
        if rms:
            self.w, self.ln, self.shift = sb("w", [KD]), sb("ln", [n]), sb("shift", [n])


def inverse_root(q, f, *waits):
    v, r, u = f.var[:, :], f.inv[:, :], f.u[:, :]
    m = q.op("act", lambda e: e.activation(f.root[:, :], v, ACT.Sqrt), *waits)
    m = q.op("dve", lambda e: e.reciprocal(r, f.root[:, :]), m)
    m = q.op("dve", lambda e: e.tensor_tensor(u, r, r, ALU.mult), m)
    m = q.op("dve", lambda e: e.tensor_tensor(u, u, v, ALU.mult), m)
    m = q.op("dve", lambda e: e.tensor_scalar(u, u, -0.5, 1.5, ALU.mult, ALU.add), m)
    return q.op("dve", lambda e: e.tensor_tensor(r, r, u, ALU.mult), m)


def norm(k, f, n, x, yh, yl, rms=None):
    q, bank, ident = k["q"], k["bank"], k["ident"]

    def stats(of, *waits):
        ms = [q.op("dve", lambda e: e.bn_stats(f.stats[:, i, :], of(i)), *waits) for i in range(n)]
        even, odd = f.stats[:, :, 1:3], f.stats[:, :, 4:6]
        dif, mean, var = f.u[:, :], f.moments[:, :, 0], f.moments[:, :, 1]
        m = q.op("dve", lambda e: e.tensor_tensor(f.moments[:, :, :], even, odd, ALU.add), ms[-1])
        d = q.op("dve", lambda e: e.tensor_tensor(dif, even[:, :, 0], odd[:, :, 0], ALU.subtract))
        v = q.op("dve", lambda e: e.tensor_scalar(var, var, 1.0 / D, None, ALU.mult), m)
        d = q.op("dve", lambda e: e.tensor_tensor(dif, dif, dif, ALU.mult), d)
        q.op("dve", lambda e: e.tensor_scalar(mean, mean, 0.5, None, ALU.mult))
        return q.op("dve", lambda e: e.scalar_tensor_tensor(
            out=var, in0=dif, scalar=0.25, in1=var, op0=ALU.mult, op1=ALU.add), d, v)

    m = stats(x, *q.at("x"), *q.at("y read"))
    m = q.op("dve", lambda e: e.tensor_scalar(f.var[:, :], f.moments[:, :, 1], LN_EPS, None,
                                              ALU.add), m)
    m = inverse_root(q, f, m)
    if rms is not None:
        got = q.load("small", lambda e: e.dma_start(f.w[:, :], rms))
        ln = q.op("dve", lambda e: e.tensor_copy(f.ln[:, :], f.inv[:, :]), m)
        m = q.op("dve", lambda e: e.tensor_tensor(f.var[:, :], f.moments[:, :, 1], f.inv[:, :], ALU.mult), m)
        m = q.op("dve", lambda e: e.tensor_tensor(f.var[:, :], f.var[:, :], f.inv[:, :], ALU.mult), m)
        m = q.op("dve", lambda e: e.tensor_scalar(f.var[:, :], f.var[:, :], RMS_EPS, None, ALU.add), m)
        m = inverse_root(q, f, m)
        m = q.op("dve", lambda e: e.tensor_tensor(f.inv[:, :], f.inv[:, :], f.ln[:, :], ALU.mult), m)
        neg = q.op("dve", lambda e: e.scalar_tensor_tensor(
            out=f.shift[:, :], in0=f.moments[:, :, 0], scalar=-1.0, in1=f.ln[:, :], op0=ALU.mult, op1=ALU.mult))
        shifted = q.op("dve", lambda e: e.tensor_scalar(f.ln[:, :], f.ln[:, :], 1.0, None, ALU.add), m, neg)
        q.wait("act", got)
        q.wait("dve", got)
    slots = len(f.y)
    ys = []

    def centre(i):
        ys.append(q.op("dve", lambda e: e.tensor_scalar(f.y[i % slots], x(i), f.moments[:, i, 0:1],
                                                        f.inv[:, i:i + 1], ALU.subtract, ALU.mult),
                       m_inv, *q.at(f"ny{i % slots} read")))

    m_inv = m
    for i in range(min(n, slots)):
        centre(i)
    last = None
    for i in range(n):
        b = i % 4
        for c in range(KD):
            m = q.op("pe", lambda e: e.transpose(bank[b][:, c * P:(c + 1) * P],
                                                 f.y[i % slots][:, c * P:(c + 1) * P], ident[:, :]),
                     ys[i], *q.at(f"bank{b} read"))
        q.note(f"ny{i % slots} read", m)
        ts = slice(i * P, i * P + P)
        src = bank[b][:, :].rearrange("p (c t) -> p c t", c=KD)
        if rms is None:
            last = split(q, "dve", yh[:, :, ts], yl[:, :, ts], src, m, *q.at("y read"))
        else:
            for c in range(KD):
                m = q.op("act", lambda e: e.activation(yh[:, c, ts], src[:, c, :], ACT.Copy,
                                                       scale=f.w[:, c:c + 1]), m)
            for c in range(KD):
                last = q.op("dve", lambda e: e.scalar_tensor_tensor(
                    out=yl[:, c, ts], in0=src[:, c, :], scalar=f.w[:, c:c + 1],
                    in1=yh[:, c, ts].bitcast(F32), op0=ALU.mult, op1=ALU.subtract), m)
        q.note(f"bank{b} read", last)
        if i + slots < n:
            centre(i + slots)
    q.note("y", last)
    if rms is not None:
        for i in range(n):
            m = q.op("pool", lambda e: e.tensor_scalar(x(i), x(i), f.ln[:, i:i + 1], f.shift[:, i:i + 1],
                                                       ALU.mult, ALU.add), shifted, ys[i])
        q.note("x", m)


def norm_all(k, name):
    with ExitStack() as s:
        norm(k, NormBuffers(k, s, name, NT), NT, lambda i: k["X"][:, i, :], k["YH"], k["YL"])
        k["q"].fence()


def attention(k, name, w_qkv, w_out, heads, qtiles, hd, rotary=None, rms=None):
    q, bank, X, YH, YL = k["q"], k["bank"], k["X"], k["YH"], k["YL"]
    ident, identb, causal = k["ident"], k["identb"], k["causal"]
    scale = float(hd) ** -0.5
    steps = D // P if qtiles == 1 else 4
    s = ExitStack()
    sb = lambda nm, shape, dt=F32: k["sb"](f"{name}_{nm}", shape, dt, s)
    cols = (qtiles + 2) * P
    raw = sb("raw", [KD, max(cols, 512)])
    WH, WL = sb("WH", [qtiles + 3, KD, P], F32R), sb("WL", [qtiles + 3, KD, P], F32R)
    o_tile = lambda r: qtiles + 2 if r == 0 else r - 1
    QH, QL = sb("QH", [qtiles, NTOK], F32R), sb("QL", [qtiles, NTOK], F32R)
    KH, KL = sb("KH", [heads, NTOK], F32R), sb("KL", [heads, NTOK], F32R)
    VH, VL = sb("VH", [heads, NT, P], F32R), sb("VL", [heads, NT, P], F32R)
    SLOTS = 3
    E = [sb(f"E{i}", [1280]) for i in range(SLOTS)]
    PHL = sb("PHL", [4, 1280], F32R)
    PH, PL = [PHL[:, i, :] for i in range(2)], [PHL[:, 2 + i, :] for i in range(2)]
    top, total, inv = sb("top", [SLOTS, 4]), sb("total", [SLOTS, 4]), sb("inv", [SLOTS, 4])
    if rotary is not None:
        swapped = [sb(f"swapped{i}", [NTOK]) for i in range(2)]
        cos_sin = sb("cos_sin", [2, T])
        q.load("small", lambda e: e.dma_start(cos_sin[:, :, :], rotary))
    for z in (KH, KL):
        m = q.op("pool", lambda e: e.memset(z[:, :, :].bitcast(F32), 0.0))
    q.note("K read", m)
    for z in (VH, VL):
        m = q.op("pool", lambda e: e.memset(z[:, :, :, :].bitcast(F32), 0.0))
    q.note("V read", m)
    f = NormBuffers(k, s, f"{name}_n", NT, [E[i][:, a * D:(a + 1) * D] for i in range(SLOTS) for a in range(2)],
                    rms is not None)
    norm(k, f, NT, lambda i: X[:, i, :], YH, YL, rms)
    ym = q.at("y")
    for i in range(SLOTS):
        q.note(f"E{i} read", *ym)
    e_at = [0, 128, 384, 768]
    chunks = [[(3, 0)], [(2, 0), (0, 384)], [(1, 0)]]
    p_at = [0, 512, 1024, 896]
    tchunks = [[(0, 0)], [(1, 0), (3, 384)], [(2, 0)]]
    p_chunk = [(0, 512), (512, 512), (1024, 256)]
    SR, TR, OB = 4, 3, 7

    head_rows = [(h, slice(h * hd, h * hd + hd)) for h in range(heads)]
    queries = [qtiles - 1] + list(range(qtiles - 1))
    order = [qtiles] + queries
    slot = lambda c: order.index(c) % 2

    def body(j):
        w_in = q.load("w", lambda e: e.dma_start(raw[:, :, 0:cols], w_qkv[j]), *q.at("raw read"))
        ready = {}
        for c in order + [qtiles + 1]:
            a = slice(c * P, c * P + P)
            ready[c] = split(q, "pool", WH[:, c, :, :], WL[:, c, :, :], raw[:, :, a], w_in,
                             *q.at(f"W{c} read"))
        q.note("raw read", ready[qtiles + 1])
        w = lambda c, kk: (WH[:, c, kk, :], WL[:, c, kk, :])
        y = lambda kk, a: (YH[:, kk, a], YL[:, kk, a])
        n = 0
        done = {}

        def rotate(c):
            f, o, rot = E[slot(c)], swapped[slot(c)], E[2]
            half = [slice(b * T, b * T + T) for b in range(B)]
            for a in half:
                p2 = q.op("pool", lambda e: e.tensor_tensor(o[:, a], o[:, a], cos_sin[:, 1, :],
                                                            ALU.mult), turned[c])
                p1 = q.op("dve", lambda e: e.tensor_tensor(rot[:, a], f[:, a], cos_sin[:, 0, :],
                                                           ALU.mult), turned[c], *q.at("E2 read"))
            p3 = q.op("dve", lambda e: e.tensor_tensor(rot[:, 0:NTOK], rot[:, 0:NTOK], o[:, :], ALU.add),
                      p1, p2)
            to = [(QH[:, c, :], QL[:, c, :], slice(0, P))] if c < qtiles else [
                (KH[ps, h, :], KL[ps, h, :], ps) for h, ps in head_rows]
            by = scale if c < qtiles else 1.0
            free = q.at(f"Q{c} read" if c < qtiles else "K read")
            his = [(a, hi, lo, ps, q.op("act", lambda e: e.activation(
                hi[:, a], rot[ps, a], ACT.Copy, scale=by), p3, *free)) for a in half for hi, lo, ps in to]
            for a, hi, lo, ps, m in his:
                m = q.op("dve", lambda e: e.scalar_tensor_tensor(
                    out=lo[:, a], in0=rot[ps, a], scalar=by, in1=hi[:, a].bitcast(F32), op0=ALU.mult,
                    op1=ALU.subtract), m)
            done[c, 0] = done[c, 1] = m
            q.note(f"E{slot(c)} read", p1)
            q.note("E2 read", m)
            q.note(f"swapped{slot(c)} read", p3)

        turned = {}

        def projected(c, b):
            nonlocal n
            bk, n = n % 8, n + 1
            a = slice(b * T, b * T + T)
            m = product(q, bank[bk][:, :], [w(c, kk) for kk in range(KD)], [y(kk, a) for kk in range(KD)],
                        ready[c], *ym, *q.at(f"bank{bk} read"))
            q.note(f"W{c} read", m)
            return bk, m

        def tile(c):
            for b in range(B):
                bk, m = projected(c, b)
                a = slice(b * T, b * T + T)
                if c < qtiles:
                    done[c, b] = split(q, "dve", QH[:, c, a], QL[:, c, a], bank[bk][:, :], m,
                                       *q.at(f"Q{c} read"), scale=scale)
                else:
                    done[c, b] = splits(q, "dve", [(KH[ps, h, a], KL[ps, h, a], bank[bk][ps, :])
                                                   for h, ps in head_rows], m, *q.at("K read"))
                q.note(f"bank{bk} read", done[c, b])

        def tile_to_rotate(c):
            f = E[slot(c)]
            for b in range(B):
                bk, m = projected(c, b)
                m = q.op("act", lambda e: e.activation(f[:, b * T:b * T + T], bank[bk][:, :], ACT.Copy), m,
                         *q.at(f"E{slot(c)} read"))
                q.note(f"bank{bk} read", m)
            for x in range(4):
                turned[c] = q.load(f"turn{slot(c)}", lambda e: e.dma_start(
                    swapped[slot(c)][32 * x:32 * x + 32, :], f[32 * (x ^ 1):32 * (x ^ 1) + 32, 0:NTOK]),
                    m, *q.at(f"swapped{slot(c)} read"))

        def values_of(b, bk):
            for i in range(TT):
                g = b * TT + i
                m = product(q, bank[bk][:, i * P:(i + 1) * P],
                            [y(kk, slice(g * P, g * P + P)) for kk in range(KD)],
                            [w(qtiles + 1, kk) for kk in range(KD)], ready[qtiles + 1],
                            *q.at(f"bank{bk} read"))
            src = bank[bk][:, :].rearrange("p (i c) -> p i c", i=TT)
            bs = slice(b * TT, b * TT + TT)
            done["v", b] = splits(q, "dve", [(VH[:, h, bs, cs], VL[:, h, bs, cs], src[:, :, cs])
                                             for h, cs in head_rows], m, *q.at("V read"))
            q.note(f"bank{bk} read", done["v", b])
            q.note(f"W{qtiles + 1} read", m)

        if rotary is None:
            for c in order:
                tile(c)
        else:
            for x, c in enumerate(order):
                tile_to_rotate(c)
                if x >= 1:
                    rotate(order[x - 1])
        for b in range(B):
            values_of(b, (n + b) % 8)
        wo_in = q.load("w2", lambda e: e.dma_start(raw[:, 0:qtiles, 0:D], w_out[j]), *q.at("raw read"))

        jobs = [(b, r, h) for b in range(B) for r in queries for h in range(heads)]
        S, EX, NRM, TP, OUT, sbank = {}, {}, {}, {}, {}, {}
        taken, wo = 0, []

        def ring():
            nonlocal taken
            taken += 1
            return (taken - 1) % SR

        o = lambda x, r: x[:, o_tile(r), :, :].rearrange("p k n -> p (k n)")

        def output_weights(r):
            wo.append(split(q, "pool", o(WH, r), o(WL, r), raw[:, r, 0:D], wo_in,
                            *q.at(f"W{o_tile(r)} read")))
            q.note("raw read", *wo)

        def output(g):
            bk = ring()
            a = slice(g * P, g * P + P)
            m = product(q, bank[bk][:, :], [(QH[:, r, a], QL[:, r, a]) for r in range(qtiles)],
                        [(o(WH, r), o(WL, r)) for r in range(qtiles)], *wo,
                        *[OUT[r, g // TT] for r in range(qtiles)], *q.at(f"bank{bk} read"))
            add = q.op("dve", lambda e: e.tensor_tensor(X[:, g, :], bank[bk][:, :], X[:, g, :],
                                                        ALU.add), m, *q.at("x"))
            q.note(f"bank{bk} read", add)
            return m, add

        def scores(n):
            b, r, h = jobs[n]
            for ci, chunk in enumerate(chunks):
                bk = sbank[n, ci] = ring()
                for i, off in chunk:
                    w_ = P * (i + 1)
                    qs = slice(b * T + i * P, b * T + i * P + P)
                    ks = slice(b * T, b * T + w_)
                    product(q, bank[bk][:, off:off + w_], [(QH[:, r, qs], QL[:, r, qs])],
                            [(KH[:, h, ks], KL[:, h, ks])], done[r, b], done[qtiles, b],
                            *q.at(f"bank{bk} read"), last=False)
                    S[n, ci] = q.op("pe", lambda e: e.matmul(
                        bank[bk][:, off + i * P:off + w_], identb[:, :], causal[:, :],
                        start=False, stop=True))

        def softmax(n):
            sl = (n + 1) % SLOTS
            for ci, chunk in enumerate(chunks):
                bk = sbank[n, ci]
                for i, off in chunk:
                    m = q.op("dve", lambda e: e.tensor_reduce(
                        top[:, sl, i:i + 1], bank[bk][:, off:off + P * (i + 1)], AX.X, ALU.max,
                        negate=True), S[n, ci], *EX.get(n - SLOTS, ()))
                for i, off in chunk:
                    m = q.op("act", lambda e: e.activation(
                        E[sl][:, e_at[i]:e_at[i] + P * (i + 1)], bank[bk][:, off:off + P * (i + 1)],
                        ACT.Exp, bias=top[:, sl, i:i + 1], accum_out=total[:, sl, i:i + 1]),
                        m, *(q.at(f"E{sl} read")))
                q.note(f"bank{bk} read", m)
            EX[n] = (m,)

        def normalise(n):
            sl = (n + 1) % SLOTS
            m = q.op("dve", lambda e: e.reciprocal(inv[:, sl, :], total[:, sl, :]), *EX[n],
                     *NRM.get((n - SLOTS, 3), ()), *q.at(f"inv{sl} read"))
            for i in range(TT):
                a = slice(e_at[i], e_at[i] + P * (i + 1))
                NRM[n, i] = (q.op("pool", lambda e: e.tensor_scalar(
                    E[sl][:, a], E[sl][:, a], inv[:, sl, i:i + 1], 0.0, ALU.mult, ALU.add), m),)
            q.note(f"inv{sl} read", *NRM[n, 3])

        def transposes(n):
            sl = (n + 1) % SLOTS
            for ci, chunk in enumerate(tchunks):
                bk = SR + (3 * n + ci) % TR
                for sblk, off in chunk:
                    for i in range(sblk, TT):
                        at = off + (i - sblk) * P
                        m = q.op("pe", lambda e: e.transpose(
                            bank[bk][:, at:at + P],
                            E[sl][:, e_at[i] + sblk * P:e_at[i] + (sblk + 1) * P], ident[:, :]),
                            *NRM[n, i], *q.at(f"bank{bk} read"))
                at, size = p_chunk[ci]
                a = slice(at, at + size)
                TP[n, ci] = split(q, "dve", PH[n % 2][:, a], PL[n % 2][:, a], bank[bk][:, 0:size],
                                  m, *q.at(f"P{n % 2} read"))
                q.note(f"bank{bk} read", TP[n, ci])
            q.note(f"E{sl} read", m)

        def values(n):
            b, r, h = jobs[n]
            for ci, chunk in enumerate(tchunks):
                for sblk, _ in chunk:
                    w_ = T - sblk * P
                    a = slice(p_at[sblk], p_at[sblk] + w_)
                    v = (VH[:, h, b * TT + sblk, :], VL[:, h, b * TT + sblk, :])
                    m = product(q, bank[OB][:, sblk * P:T], [v], [(PH[n % 2][:, a], PL[n % 2][:, a])],
                                TP[n, ci], done["v", b], *(q.at("bank7 read") if h == 0 else ()),
                                first=h == 0 and sblk == 0, last=h == heads - 1 and ci == 2)
            q.note(f"P{n % 2} read", m)
            if h == heads - 1:
                a = slice(b * T, b * T + T)
                OUT[r, b] = split(q, "dve", QH[:, r, a], QL[:, r, a], bank[OB][:, :], m)
                q.note("bank7 read", OUT[r, b])

        J = len(jobs)
        between = {12: 0, 14: 1, 16: 2, 17: 3} if J == 16 else {7: 0, 8: 1, 9: 2, 10: 3}
        for n in range(J + 3):
            if n < J:
                scores(n)
                softmax(n)
            if n == 0 and rotary is not None:
                rotate(order[-1])
            if 2 <= n < 2 + qtiles:
                output_weights(n - 2)
            if 1 <= n <= J:
                normalise(n - 1)
            if 2 <= n < J + 2:
                transposes(n - 2)
            if n in between:
                output(between[n])
            if n >= 3:
                values(n - 3)
        q.note("K read", S[J - 1, 2])
        q.note("V read", *q.at(f"P{(J - 1) % 2} read"))
        for g in range(TT, NT):
            m, add = output(g)
        q.note("x", add)
        for r in range(qtiles):
            q.note(f"W{o_tile(r)} read", m)
            q.note(f"Q{r} read", m)

    q.loop(steps, body)
    q.fence()
    s.close()


def memory_attention(k, ctxT, ctx_rows, mask):
    q, bank, X = k["q"], k["bank"], k["X"]
    ident, identb = k["ident"], k["identb"]
    scale = float(D) ** -0.5
    s = ExitStack()
    sb = lambda nm, shape, dt=F32: k["sb"](f"m_{nm}", shape, dt, s)
    half = CT // 2
    raw = sb("raw", [KD, SC])
    rraw = raw[:, :, :].rearrange("p k n -> p (k n)").rearrange("p (c d) -> p c d", d=D)
    CH, CL = sb("CH", [KD, SC], F32R), sb("CL", [KD, SC], F32R)
    RH, RL = sb("RH", [CT, D], F32R), sb("RL", [CT, D], F32R)
    ma = sb("ma", [SC], U8)
    mf, mb = sb("mf", [SC]), sb("mb", [SC], BF16)
    ones, valid = sb("ones", [P], BF16), sb("valid", [1])
    E = [sb(f"E{i}", [SC]) for i in range(2)]
    PH, PL = [sb(f"PH{i}", [SC], F32R) for i in range(2)], [sb(f"PL{i}", [SC], F32R) for i in range(2)]
    top, total = sb("top", [TT, 2]), sb("total", [TT, 2])
    nb, inv = sb("nb", [TT]), sb("inv", [TT])
    z = q.op("pool", lambda e: e.memset(ones[:, :], 0.0))
    q.op("pool", lambda e: e.memset(ones[0:1, :], 1.0), z)
    q.fence()

    def body(b):
        c_in = q.load("ctx", lambda e: e.dma_start(raw[:, :, :], ctxT[b]), *q.at("raw read"))
        m_in = q.load("small", lambda e: e.dma_start(
            ma[:, :], mask[b].rearrange("(a n) -> a n", a=1).broadcast_to([P, SC])), *q.at("mask read"))
        for kk in range(KD):
            cm = split(q, "dve", CH[:, kk, :], CL[:, kk, :], raw[:, kk, :], c_in, *q.at("C read"))
        r_in = q.load("ctx", lambda e: e.dma_start(rraw, ctx_rows[b]), cm)
        m = q.op("dve", lambda e: e.tensor_copy(mf[:, :], ma[:, :]), m_in, *q.at("mask read"))
        v = q.op("dve", lambda e: e.tensor_reduce(valid[:, :], mf[:, :], AX.X, ALU.max), m)
        mm = q.op("dve", lambda e: e.tensor_scalar(mb[:, :], mf[:, :], -MASKED, MASKED, ALU.mult,
                                                   ALU.add), m)
        norm(k, f, TT, lambda i: X[:, bass.ds(b * TT + i, 1), :].rearrange("p a d -> p (a d)"), NH, NL)
        ym = q.at("y")
        for c in range(CT):
            rm = split(q, "dve", RH[:, c, :], RL[:, c, :], rraw[:, c, :], r_in, *q.at("R read"))
        q.note("raw read", rm)
        EX, TP = {}, {}

        def scores(i):
            for h in range(2):
                bk = (2 * i + h) % 4
                a = slice(h * 512, h * 512 + 512)
                ts = slice(i * P, i * P + P)
                product(q, bank[bk][:, :], [(NH[:, kk, ts], NL[:, kk, ts]) for kk in range(KD)],
                        [(CH[:, kk, a], CL[:, kk, a]) for kk in range(KD)], cm, *ym,
                        *q.at(f"bank{bk} read"), last=False)
                sm = q.op("pe", lambda e: e.matmul(bank[bk][:, :], ones[:, :], mb[:, a], start=False,
                                                   stop=True), mm)
                m = q.op("dve", lambda e: e.tensor_reduce(top[:, i, h:h + 1], bank[bk][:, :], AX.X,
                                                          ALU.max), sm, *q.at("top read"))
            m = q.op("dve", lambda e: e.tensor_reduce(nb[:, i:i + 1], top[:, i, :], AX.X, ALU.max,
                                                      negate=True), m)
            m = q.op("dve", lambda e: e.tensor_scalar(nb[:, i:i + 1], nb[:, i:i + 1], scale, None,
                                                      ALU.mult), m)
            for h in range(2):
                bk = (2 * i + h) % 4
                a = slice(h * 512, h * 512 + 512)
                EX[i] = q.op("act", lambda e: e.activation(
                    E[i % 2][:, a], bank[bk][:, :], ACT.Exp, bias=nb[:, i:i + 1], scale=scale,
                    accum_out=total[:, i, h:h + 1]), m, *q.at(f"mE{i % 2} read"))
                q.note(f"bank{bk} read", EX[i])
            return sm

        def readout(i):
            m = q.op("dve", lambda e: e.tensor_tensor(inv[:, i:i + 1], total[:, i, 0:1],
                                                      total[:, i, 1:2], ALU.add), EX[i])
            m = q.op("dve", lambda e: e.reciprocal(inv[:, i:i + 1], inv[:, i:i + 1]), m)
            im = q.op("dve", lambda e: e.tensor_tensor(inv[:, i:i + 1], inv[:, i:i + 1],
                                                       valid[:, :], ALU.mult), m, v)
            for h in range(2):
                bk = 4 + h
                for c in range(half):
                    m = q.op("pe", lambda e: e.transpose(
                        bank[bk][:, c * P:(c + 1) * P],
                        E[i % 2][:, (h * half + c) * P:(h * half + c + 1) * P], ident[:, :]),
                        EX[i], *q.at(f"bank{bk} read"))
                a = slice(h * 512, h * 512 + 512)
                TP[i] = split(q, "dve", PH[i % 2][:, a], PL[i % 2][:, a], bank[bk][:, :], m,
                              *q.at(f"mP{i % 2} read"))
                q.note(f"bank{bk} read", TP[i])
            q.note(f"mE{i % 2} read", m)
            return im

        def out(i, im):
            bk = 6 + i % 2
            m = product(q, bank[bk][:, :],
                        [(PH[i % 2][:, c * P:(c + 1) * P], PL[i % 2][:, c * P:(c + 1) * P])
                         for c in range(CT)],
                        [(RH[:, c, :], RL[:, c, :]) for c in range(CT)], TP[i], rm,
                        *q.at(f"bank{bk} read"))
            q.note(f"mP{i % 2} read", m)
            xs = X[:, bass.ds(b * TT + i, 1), :].rearrange("p a d -> p (a d)")
            add = q.op("dve", lambda e: e.scalar_tensor_tensor(
                out=xs, in0=bank[bk][:, :], scalar=inv[:, i:i + 1], in1=xs, op0=ALU.mult,
                op1=ALU.add), m, im)
            q.note(f"bank{bk} read", add)
            return m, add

        ims = {}
        for i in range(TT + 1):
            if i < TT:
                sm = scores(i)
            if i >= 1:
                ims[i - 1] = readout(i - 1)
                m, add = out(i - 1, ims[i - 1])
        q.note("top read", EX[TT - 1])
        q.note("C read", sm)
        q.note("mask read", sm)
        q.note("y read", sm)
        q.note("R read", m)
        q.note("x", add)

    NH, NL = sb("NH", [KD, T], F32R), sb("NL", [KD, T], F32R)
    f = NormBuffers(k, s, "m_n", TT)
    q.loop(B, body)
    q.fence()
    s.close()


def router_ranks(q, sb, name, v, shape, top, *waits):
    n = shape[-1]
    rank, ge = sb(f"{name}_rank", shape), sb(f"{name}_ge", shape)
    m = q.op("dve", lambda e: e.memset(rank[:, :, :], 0.0), *waits)
    for d in range(1, n):
        m1 = q.op("dve", lambda e: e.tensor_tensor(ge[:, :, 0:n - d], v[:, :, 0:n - d], v[:, :, d:n],
                                                   ALU.is_ge), m)
        m2 = q.op("dve", lambda e: e.tensor_tensor(rank[:, :, d:n], rank[:, :, d:n],
                                                   ge[:, :, 0:n - d], ALU.add), m1)
        m3 = q.op("dve", lambda e: e.tensor_scalar(ge[:, :, 0:n - d], ge[:, :, 0:n - d], -1.0, 1.0,
                                                   ALU.mult, ALU.add), m2)
        m = q.op("dve", lambda e: e.tensor_tensor(rank[:, :, 0:n - d], rank[:, :, 0:n - d],
                                                  ge[:, :, 0:n - d], ALU.add), m3)
    m = q.op("dve", lambda e: e.tensor_scalar(rank[:, :, :], rank[:, :, :], top - 0.5, None,
                                              ALU.is_le), m)
    return rank, m


def experts(k, name, w_up, w_down, routed, shared, gated, router, bias):
    q, bank, X, YH, YL = k["q"], k["bank"], k["X"], k["YH"], k["YL"]
    s = ExitStack()
    sb = lambda nm, shape, dt=F32: k["sb"](f"{name}_{nm}", shape, dt, s)
    E_ = routed + shared
    cols = INNER * (2 if gated else 1)
    raw, UH, UL = sb("raw", [KD, cols]), sb("UH", [KD, cols], F32R), sb("UL", [KD, cols], F32R)
    draw = sb("draw", [3, D])
    DH, DL = sb("DH", [3, D], F32R), sb("DL", [3, D], F32R)
    HH, HL = sb("HH", [3, NTOK], F32R), sb("HL", [3, NTOK], F32R)
    act = [sb(f"act{i}", [512]) for i in range(2)]
    hid = [sb(f"hid{i}", [512]) for i in range(2)]
    comb, cw = sb("comb", [NT, E_]), sb("cw", [NT])
    route(k, sb, name, router, bias, routed, shared, comb)

    def body(e_):
        up_in = q.load("w", lambda e: e.dma_start(raw[:, :, :], w_up[e_]), *q.at("raw read"))
        q.load("w2", lambda e: e.dma_start(
            draw[:, 0:2, :], w_down[e_, 0:256, :].rearrange("(k p) n -> p k n", p=P)), *q.at("draw read"))
        dn_in = q.load("w2", lambda e: e.dma_start(draw[0:96, 2, :], w_down[e_, 256:INNER, :]))
        um = split(q, "pool", UH[:, :, :], UL[:, :, :], raw[:, :, :], up_in, *q.at("U read"))
        q.note("raw read", um)
        cm = q.op("dve", lambda e: e.tensor_scalar(
            cw[:, :], comb[:, :, bass.ds(e_, 1)].rearrange("p t a -> p (t a)"), 1.0, None, ALU.mult),
            *q.at("x"))
        dm1 = split(q, "pool", DH[:, 0:2, :], DL[:, 0:2, :], draw[:, 0:2, :], dn_in, *q.at("D read"))
        dm = split(q, "pool", DH[0:96, 2, :], DL[0:96, 2, :], draw[0:96, 2, :], dn_in)
        q.note("draw read", dm)
        H = {}
        n = 0
        for b in range(B):
            ts = slice(b * T, b * T + T)
            y = [(YH[:, kk, ts], YL[:, kk, ts]) for kk in range(KD)]
            for it, (r0, rows) in enumerate(ITILES):
                gb, ub = (2 * n) % 4, (2 * n + 1) % 4
                sl = n % 2
                n += 1
                wt = lambda c: [(UH[:, kk, c:c + rows], UL[:, kk, c:c + rows]) for kk in range(KD)]
                gm = product(q, bank[gb][0:rows, :], wt(r0), y, um, *q.at(f"bank{gb} read"))
                if gated:
                    pm = product(q, bank[ub][0:rows, :], wt(INNER + r0), y, *q.at(f"bank{ub} read"))
                else:
                    pm = gm
                am = q.op("act", lambda e: e.activation(act[sl][0:rows, :], bank[gb][0:rows, :],
                                                        ACT.Silu), gm, *q.at(f"act{sl} read"))
                q.note(f"bank{gb} read", am)
                src = act
                if gated:
                    am = q.op("dve", lambda e: e.tensor_tensor(
                        hid[sl][0:rows, :], bank[ub][0:rows, :], act[sl][0:rows, :], ALU.mult),
                        am, pm, *q.at(f"hid{sl} read"))
                    q.note(f"bank{ub} read", am)
                    q.note(f"act{sl} read", am)
                    src = hid
                H[it, b] = split(q, "dve", HH[0:rows, it, ts], HL[0:rows, it, ts],
                                 src[sl][0:rows, :], am, *q.at(f"H{b} read"))
                q.note(f"{'hid' if gated else 'act'}{sl} read", H[it, b])
        q.note("U read", pm)
        for g in range(NT):
            bk = 4 + g % 4
            a = slice(g * P, g * P + P)
            m = product(q, bank[bk][:, :],
                        [(HH[0:rows, it, a], HL[0:rows, it, a]) for it, (_, rows) in enumerate(ITILES)],
                        [(DH[0:rows, it, :], DL[0:rows, it, :]) for it, (_, rows) in enumerate(ITILES)],
                        dm1, dm, *[H[it, g // TT] for it in range(3)], *q.at(f"bank{bk} read"))
            add = q.op("dve", lambda e: e.scalar_tensor_tensor(
                out=X[:, g, :], in0=bank[bk][:, :], scalar=cw[:, g:g + 1], in1=X[:, g, :],
                op0=ALU.mult, op1=ALU.add), m, cm)
            q.note(f"bank{bk} read", add)
            q.note(f"H{g // TT} read", m)
        q.note("D read", m)
        q.note("x", add)

    q.loop(E_, body)
    q.fence()
    s.close()


def route(k, sb, name, router, bias, routed, shared, comb):
    q, bank, YH, YL = k["q"], k["bank"], k["YH"], k["YL"]
    R = routed
    raw = sb("rw", [KD, R])
    RH, RL = sb("rh", [KD, R], F32R), sb("rl", [KD, R], F32R)
    sc = sb("sc", [NT, R])
    den = sb("den", [NT])
    got = q.load("small", lambda e: e.dma_start(raw[:, :, :], router.rearrange("(k p) n -> p k n", p=P)))
    m = split(q, "dve", RH[:, :, :], RL[:, :, :], raw[:, :, :], got)
    for g in range(NT):
        a = slice(g * P, g * P + P)
        m = product(q, bank[0][:, g * R:(g + 1) * R], [(YH[:, kk, a], YL[:, kk, a]) for kk in range(KD)],
                    [(RH[:, kk, :], RL[:, kk, :]) for kk in range(KD)], m)
    logits = bank[0][:, 0:NT * R].rearrange("p (t r) -> p t r", r=R)
    if bias is not None:
        G, TOPG, TOPK, FACTOR = 4, 2, 6, 2.5
        S_ = R // G
        bs, ch = sb("bs", [R]), sb("ch", [NT, R])
        pair, gs, gt = sb("pair", [NT * G, 6]), sb("gs", [NT, G]), sb("gt", [NT * G, S_])
        bm = q.load("w2", lambda e: e.dma_start(
            bs[:, :], bias.rearrange("(a n) -> a n", a=1).broadcast_to([P, R])))
        sm = q.op("act", lambda e: e.activation(sc[:, :, :], logits, ACT.Sigmoid), m)
        m = q.op("dve", lambda e: e.tensor_tensor(
            ch[:, :, :], sc[:, :, :], bs[:, :].rearrange("p (a r) -> p a r", a=1).broadcast_to([P, NT, R]),
            ALU.add), sm, bm)
        c4 = ch[:, :, :].rearrange("p t (g s) -> p (t g) s", g=G)
        at = 0
        for d in range(1, S_):
            pm = q.op("dve", lambda e: e.tensor_tensor(pair[:, :, at:at + S_ - d], c4[:, :, 0:S_ - d],
                                                       c4[:, :, d:S_], ALU.add), m)
            at += S_ - d
        gm = q.op("dve", lambda e: e.tensor_reduce(gs[:, :, :].rearrange("p t g -> p (t g)"),
                                                   pair[:, :, :], AX.X, ALU.max), pm)
        group, gm = router_ranks(q, sb, f"{name}_g", gs, [NT, G], TOPG, gm)
        gf = group[:, :, :].rearrange("p t g -> p (t g)")
        tm = q.op("dve", lambda e: e.tensor_tensor(
            gt[:, :, :], c4, gf.rearrange("p (n a) -> p n a", a=1).broadcast_to([P, NT * G, S_]),
            ALU.mult), gm)
        chosen, m = router_ranks(q, sb, f"{name}_e", gt[:, :, :].rearrange("p (t g) s -> p t (g s)", g=G),
                                 [NT, R], TOPK, tm)
    else:
        TOPK, FACTOR = 2, 1.0
        mx = sb("mx", [NT])
        bc = lambda a: a.rearrange("p (t a) -> p t a", a=1).broadcast_to([P, NT, R])
        m = q.op("dve", lambda e: e.tensor_reduce(mx[:, :], logits, AX.X, ALU.max), m)
        m = q.op("dve", lambda e: e.tensor_tensor(sc[:, :, :], logits, bc(mx[:, :]), ALU.subtract), m)
        m = q.op("act", lambda e: e.activation(sc[:, :, :], sc[:, :, :], ACT.Exp), m)
        m = q.op("dve", lambda e: e.tensor_reduce(den[:, :], sc[:, :, :], AX.X, ALU.add), m)
        m = q.op("dve", lambda e: e.reciprocal(den[:, :], den[:, :]), m)
        m = q.op("dve", lambda e: e.tensor_tensor(sc[:, :, :], sc[:, :, :], bc(den[:, :]), ALU.mult), m)
        chosen, m = router_ranks(q, sb, f"{name}_e", sc, [NT, R], TOPK, m)
    m = q.op("dve", lambda e: e.tensor_tensor(sc[:, :, :], sc[:, :, :], chosen[:, :, :], ALU.mult), m)
    m = q.op("dve", lambda e: e.tensor_reduce(den[:, :], sc[:, :, :], AX.X, ALU.add), m)
    if bias is not None:
        m = q.op("dve", lambda e: e.tensor_scalar(den[:, :], den[:, :], 1e-20, None, ALU.add), m)
    m = q.op("dve", lambda e: e.reciprocal(den[:, :], den[:, :]), m)
    if FACTOR != 1.0:
        m = q.op("dve", lambda e: e.tensor_scalar(den[:, :], den[:, :], FACTOR, None, ALU.mult), m)
    m = q.op("dve", lambda e: e.tensor_tensor(
        comb[:, :, shared:shared + R], sc[:, :, :],
        den[:, :].rearrange("p (t a) -> p t a", a=1).broadcast_to([P, NT, R]), ALU.mult), m)
    q.op("dve", lambda e: e.memset(comb[:, :, 0:shared], 1.0))
    q.fence()


def linear_attention(k, t):
    q, bank, X, YH, YL = k["q"], k["bank"], k["X"], k["YH"], k["YL"]
    ident = k["ident"]
    HN, HD, FD = 16, 32, 64
    G = P // HD
    VA = HD + 1
    NP_ = HN // 2
    s = ExitStack()
    sb = lambda nm, shape, dt=F32: k["sb"](f"lin_{nm}", shape, dt, s)
    raw = sb("raw", [KD, D])
    W1, W2 = ((sb(f"W{i}H", [KD, D], F32R), sb(f"W{i}L", [KD, D], F32R)) for i in (1, 2))
    W = {"k": W1, "v": W2, "q": W1, "o": W2}
    FR = [sb(f"FR{i}", [G * FD]) for i in range(2)]
    F = {w: (sb(f"F{w}H", [G * FD], F32R), sb(f"F{w}L", [G * FD], F32R)) for w in "qk"}
    bq, bk, bv, bo = sb("bq", [KD]), sb("bk", [KD]), sb("bv", [D]), sb("bo", [D])
    am = sb("am", [CT])
    craw = sb("craw", [KD, 512])
    CH, CL = sb("CH", [KD, SC], F32R), sb("CL", [KD, SC], F32R)
    KH, KL = sb("KH", [KD, T], F32R), sb("KL", [KD, T], F32R)
    kf = sb("kf", [HN * FD])
    kfH, kfL = ([sb(f"kf{x}{i}", [HN * FD], F32R) for i in range(2)] for x in "HL")
    v = sb("v", [HN, VA])
    vHL = [sb(f"vHL{i}", [2, HN, VA], F32R) for i in range(2)]
    acc, zero = sb("acc", [B * NP_, 2, 2 * VA]), sb("zero", [D])
    zerob = sb("zerob", [3 * 4 * VA], BF16)
    pairs = {5: (0, 1, 2), 6: (3, 4, 5), 7: (6, 7)}
    kvH, kvL = sb("kvH", [B * NP_, 2 * VA], F32R), sb("kvL", [B * NP_, 2 * VA], F32R)
    qfH, qfL = (c[:, :, :].rearrange("p k (a t) -> p (k a) t", t=T) for c in (CH, CL))
    den = sb("den", [2, HN])
    o = [kf[:, i * D:(i + 1) * D] for i in range(2)]
    oH, oL = ([x[0][:, i * D:(i + 1) * D].rearrange("p (c t) -> p c t", c=KD) for i in range(2)] for x in (kfH, kfL))
    f = NormBuffers(k, s, "lin_n", NT, [kf[:, i * D:(i + 1) * D] for i in range(2)] + [bo[:, :], zero[:, :]])

    def weights(x, eng, *free):
        m = q.load("w", lambda e: e.dma_start(
            raw[:, :, :], t[f"l_{x}"].rearrange("(k p) n -> p k n", p=P)), *q.at("raw read"))
        for kk in range(KD):
            m2 = split(q, eng, W[x][0][:, kk, :], W[x][1][:, kk, :], raw[:, kk, :], m, *free)
        q.note("raw read", m2)
        return m2

    w = lambda x, kk, a: (W[x][0][:, kk, a], W[x][1][:, kk, a])
    q.load("small", lambda e: e.dma_start(bq[:, :], t["l_bq"]))
    q.load("small", lambda e: e.dma_start(bk[:, :], t["l_bk"]))
    everywhere = lambda to, of, *waits: q.load("small", lambda e: e.dma_start(
        to[:, :], t[of].rearrange("(a n) -> a n", a=1).broadcast_to([P, D])), *waits)
    small = everywhere(bv, "l_bv")
    fr = {}
    for i, x in enumerate("kq"):
        m = q.op("pool", lambda e: e.memset(FR[i][:, :], 0.0))
        for g in range(G):
            fr[x] = q.load(("w2", "turn0")[i], lambda e: e.dma_start(
                FR[i][g * HD:(g + 1) * HD, g * FD:(g + 1) * FD], t[f"l_{x}f"]), m)
    q.op("pool", lambda e: e.memset(v[:, :, HD:VA], 1.0))
    z = q.op("pool", lambda e: e.memset(zerob[:, :], 0.0))
    for kv in (kvH, kvL):
        kvz = q.op("pool", lambda e: e.memset(kv[:, :, :].bitcast(F32), 0.0))
    for i, x in enumerate("kq"):
        fs = split(q, "pool", F[x][0][:, :], F[x][1][:, :], FR[i][:, :], fr[x])
    for e_ in ("act", "dve", "pe", "pool"):
        q.wait(e_, small, z, kvz, fs)
    wk = weights("k", "pool")
    norm(k, f, NT, lambda i: X[:, i, :], YH, YL)
    q.note("kf read", *q.at("y"))
    bo_in = everywhere(bo, "l_bo", *q.at("y"))
    z = q.op("pool", lambda e: e.memset(zero[:, :], 0.0), *q.at("y"))
    q.wait("dve", bo_in, z)
    wv = weights("v", "dve")

    def keys_values(b):
        small = q.load("small", lambda e: e.dma_start(am[:, :], t["l_mask"][b]), *q.at("am read"))
        vm, fm, km = {}, {}, {}

        def context(h):
            hs = slice(h * 512, h * 512 + 512)
            m = q.load("ctx", lambda e: e.dma_start(craw[:, :, :], t["ctxT"][b, :, :, hs]), *q.at("craw read"))
            ms = []
            for kk in range(KD):
                cm = split(q, ("dve", "pool")[kk % 2], CH[:, kk, hs], CL[:, kk, hs], craw[:, kk, :], m, *q.at(f"C{h} read"))
                ms.append(cm)
            q.note("craw read", *ms[-2:])
            return ms[-2:]

        def keys(h):
            hs = slice(h * 512, h * 512 + 512)
            for c in range(KD):
                m = product(q, bank[c][:, :], [w("k", kk, slice(c * P, c * P + P)) for kk in range(KD)],
                            [(CH[:, kk, hs], CL[:, kk, hs]) for kk in range(KD)], wk, *cm[h],
                            *q.at(f"bank{c} read"))
                km[c] = split(q, "dve", KH[:, c, :], KL[:, c, :], bank[c][:, :], m, *q.at("K read"),
                              bias=bk[:, c:c + 1])
                q.note(f"bank{c} read", km[c])

        def values_and_features(i):
            a = slice(i * P, i * P + P)
            ka = slice(i % 4 * P, i % 4 * P + P)
            r = 4
            m = product(q, bank[r][:, :], [(CH[:, kk, a], CL[:, kk, a]) for kk in range(KD)],
                        [w("v", kk, slice(0, D)) for kk in range(KD)], wv, *cm[i // 4], *q.at(f"bank{r} read"))
            if i % 4 == 3:
                q.note(f"C{i // 4} read", m)
            added = q.op("dve", lambda e: e.tensor_tensor(
                v[:, :, 0:HD], bank[r][:, :].rearrange("p (h e) -> p h e", e=HD),
                bv[:, :].rearrange("p (h e) -> p h e", e=HD), ALU.add), m, *q.at("v read"))
            q.note(f"bank{r} read", added)
            kfm = []
            for c in range(2):
                r = (2 * i + c) % 4
                for d in range(2):
                    m = product(q, bank[r][:, d * 256:(d + 1) * 256],
                                [(KH[:, 2 * c + d, ka], KL[:, 2 * c + d, ka])],
                                [(F["k"][0][:, :], F["k"][1][:, :])], km[2 * c + d], *q.at(f"bank{r} read"))
                fs = slice(c * 512, c * 512 + 512)
                kfm.append(q.op("dve", lambda e: e.tensor_scalar(
                    kf[:, fs], bank[r][:, :], 0.0, am[:, i:i + 1], ALU.max, ALU.mult), m, small,
                    *q.at("kf read")))
                q.note(f"bank{r} read", kfm[-1])
            q.note("K read", m)
            vm[i] = split(q, "dve", vHL[i % 2][:, 0, :, :], vHL[i % 2][:, 1, :, :], v[:, :, :], added,
                          *q.at(f"kv{i % 2} read"))
            q.note("v read", vm[i])
            for c in range(2):
                fs = slice(c * 512, c * 512 + 512)
                fm[i] = split(q, "dve", kfH[i % 2][:, fs], kfL[i % 2][:, fs], kf[:, fs], kfm[c],
                              *q.at(f"kv{i % 2} read"))
            q.note("kf read", fm[i])

        def contract(i):
            for r, ps in pairs.items():
                n = len(ps) * 4 * VA
                nothing = lambda e, at: e.matmul(bank[r][:, 0:n], k["identb"][:, :], zerob[:, 0:n],
                                                 start=at == "start", stop=at == "stop")
                if i == 0:
                    q.quiet("pe", lambda e: nothing(e, "start"), *q.at(f"bank{r} read"))
                for d, p_ in enumerate(ps):
                    fs = slice(p_ * P, p_ * P + P)
                    at = d * 4 * VA
                    both = vHL[i % 2][:, :, 2 * p_:2 * p_ + 2, :].rearrange("p x h e -> p x (h e)")
                    q.quiet("pe", lambda e: e.matmul(
                        bank[r][:, at:at + 4 * VA], kfH[i % 2][:, fs], both, start=False, stop=False,
                        skip_group_check=True), fm[i], vm[i])
                    m = q.op("pe", lambda e: e.matmul(
                        bank[r][:, at:at + 2 * VA], kfL[i % 2][:, fs], both[:, 0, :], start=False, stop=False,
                        skip_group_check=True))
                if i == CT - 1:
                    m = q.op("pe", lambda e: nothing(e, "stop"))
                    m2 = q.op("dve", lambda e: e.tensor_tensor(
                        acc[:, bass.ds(b * NP_ + ps[0], len(ps)), :, :].rearrange("p a x e -> p (a x e)"),
                        bank[r][:, 0:n], zero[:, 0:n], ALU.add), m)
                    q.note(f"bank{r} read", m2)
                    q.note("acc", m2)
            q.note(f"kv{i % 2} read", m)

        cm = {0: context(0)}
        for i in range(CT):
            if i == 2:
                cm[1] = context(1)
            if i % 4 == 0:
                keys(i // 4)
            values_and_features(i)
            if i >= 1:
                contract(i - 1)
        contract(CT - 1)
        q.note("am read", *q.at("kf read"))

    q.loop(B, keys_values)
    last = q.at("K read") + q.at("kv0 read") + q.at("kv1 read")
    wq = weights("q", "dve", *last)
    both = q.op("dve", lambda e: e.tensor_tensor(acc[:, :, 0, :], acc[:, :, 0, :], acc[:, :, 1, :], ALU.add),
                *q.at("acc"))
    for h in range(2):
        ps, es = slice(h * FD, (h + 1) * FD), slice(h * VA, (h + 1) * VA)
        kvm = split(q, "dve", kvH[ps, :, es], kvL[ps, :, es], acc[ps, :, 0, es], both)
    wo = weights("o", "pool", *last)
    ym = q.at("y")
    for e_ in ("act", "dve", "pe"):
        q.wait(e_, *last)

    def queries(b):
        QH, QL = KH, KL
        qm, pm, num, tr = {}, {}, {}, {}

        def query(c):
            r = c % 2
            m = product(q, bank[r][:, :], [w("q", kk, slice(c * P, c * P + P)) for kk in range(KD)],
                        [(YH[:, kk, bass.ds(b * T, T)], YL[:, kk, bass.ds(b * T, T)]) for kk in range(KD)],
                        wq, *ym, *q.at(f"bank{r} read"))
            qm[c] = split(q, "dve", QH[:, c, :], QL[:, c, :], bank[r][:, :], m, *q.at("Q read"),
                          bias=bq[:, c:c + 1])
            q.note(f"bank{r} read", qm[c])

        def features(c):
            for d in range(2):
                p_ = 2 * c + d
                r = 2 + p_ % 2
                m = product(q, bank[r][:, :], [(F["q"][0][:, d * P:(d + 1) * P], F["q"][1][:, d * P:(d + 1) * P])],
                            [(QH[:, c, :], QL[:, c, :])], qm[c], *q.at(f"bank{r} read"))
                hi = q.op("act", lambda e: e.activation(qfH[:, p_, :], bank[r][:, :], ACT.Relu), m,
                          *q.at("qf read"))
                pm[p_] = q.op("dve", lambda e: e.scalar_tensor_tensor(
                    out=qfL[:, p_, :], in0=bank[r][:, :], scalar=0.0, in1=qfH[:, p_, :].bitcast(F32),
                    op0=ALU.max, op1=ALU.subtract), hi)
                q.note(f"bank{r} read", pm[p_])
            if c == KD - 1:
                q.note("Q read", m)

        def readout(i):
            a = slice(i * P, i * P + P)
            for c in range(2):
                r = (4, 5, 6, 7)[(2 * i + c) % 4]
                for d in range(4):
                    p_ = 4 * c + d
                    m = product(q, bank[r][:, d * 2 * VA:(d + 1) * 2 * VA], [(qfH[:, p_, a], qfL[:, p_, a])],
                                [tuple(x[:, bass.ds(b * NP_ + p_, 1), :].rearrange("p a e -> p (a e)")
                                       for x in (kvH, kvL))], pm[p_], kvm, *q.at(f"bank{r} read"))
                hs = slice(8 * c, 8 * c + 8)
                nu = bank[r][:, 0:8 * VA].rearrange("p (h e) -> p h e", e=VA)
                dh = den[:, i % 2, hs]
                m1 = q.op("dve", lambda e: e.tensor_scalar(dh, nu[:, :, HD], 1e-8, None, ALU.add), m)
                m1 = q.op("dve", lambda e: e.reciprocal(dh, dh), m1)
                num[i] = q.op("dve", lambda e: e.tensor_tensor(
                    o[i % 2][:, 8 * c * HD:8 * (c + 1) * HD].rearrange("p (h e) -> p h e", e=HD), nu[:, :, 0:HD],
                    dh.rearrange("p (h a) -> p h a", a=1).broadcast_to([P, 8, HD]), ALU.mult), m1,
                    *q.at(f"o{i % 2} read"))
                q.note(f"bank{r} read", num[i])
            if i == TT - 1:
                q.note("qf read", m)

        def transposed(i):
            r = i % 2
            for c in range(KD):
                m = q.op("pe", lambda e: e.transpose(bank[r][:, c * P:(c + 1) * P], o[i % 2][:, c * P:(c + 1) * P],
                                                     ident[:, :]), num[i], *q.at(f"bank{r} read"))
            q.note(f"o{i % 2} read", m)
            tr[i] = split(q, "dve", oH[i % 2], oL[i % 2], bank[r][:, :].rearrange("p (c t) -> p c t", c=KD), m,
                          *q.at(f"oH{i % 2} read"))
            q.note(f"bank{r} read", tr[i])

        def project(i):
            r = 2 + i % 2
            m = product(q, bank[r][:, :], [(oH[i % 2][:, c, :], oL[i % 2][:, c, :]) for c in range(KD)],
                        [w("o", c, slice(0, D)) for c in range(KD)], tr[i], wo, *q.at(f"bank{r} read"))
            q.note(f"oH{i % 2} read", m)
            xs = X[:, bass.ds(b * TT + i, 1), :].rearrange("p a d -> p (a d)")
            x1 = q.op("dve", lambda e: e.tensor_tensor(xs, bank[r][:, :], xs, ALU.add), m)
            q.note(f"bank{r} read", x1)
            q.note("x", q.op("dve", lambda e: e.tensor_tensor(xs, xs, bo[:, :], ALU.add), x1))

        for c in range(KD + 1):
            if c < KD:
                query(c)
            if c >= 1:
                features(c - 1)
        for i in range(TT + 2):
            if i < TT:
                readout(i)
            if 1 <= i <= TT:
                transposed(i - 1)
            if i >= 2:
                project(i - 2)

    q.loop(B, queries)
    q.fence()
    s.close()


_OUT = [((B, T, D), "float32")]


def _laid_out(i):
    import numpy as np

    c = np.ascontiguousarray

    def by_rows(w):
        return w.reshape(KD, P, -1).transpose(1, 0, 2)

    def qkv(wq, wk, wv):
        return c(np.stack([np.concatenate([by_rows(x) for x in parts], axis=2) for parts in zip(wq, wk, wv)]))

    a = {}
    a["x"] = i["x"]
    ctx = i["ctx_2048"]
    a["ctxT"] = c(ctx.transpose(0, 2, 1).reshape(B, KD, P, SC).transpose(0, 2, 1, 3))
    a["ctx"] = c(ctx.reshape(B, CT, P, D).transpose(0, 2, 1, 3))
    a["mem_mask"] = i["mask_BxS2_bk0"]
    cut = [slice(j * P, j * P + P) for j in range(4)]
    q, kk, v, o = (i[f"L0_attn_W{x}"].T for x in "qkvo")
    a["a0_qkv"] = qkv([q[:, s] for s in cut], [kk[:, s] for s in cut], [v[:, s] for s in cut])
    a["a0_wo"] = c(np.stack([o[s][:, None] for s in cut]))
    w = i["L1_attn_w_in"].T
    q = w[:, :2048].reshape(D, 4, 2, 4, 64).transpose(1, 0, 3, 2, 4).reshape(4, D, 512)
    kk, v = w[:, 2048:2560], w[:, 2560:]
    a["a1_qkv"] = qkv(list(q), [kk[:, s] for s in cut], [v[:, s] for s in cut])
    o = i["L1_attn_w_out"].T.reshape(4, 2, 4, 64, D).transpose(0, 1, 3, 2, 4)
    a["a1_wo"] = c(o.reshape(4, P, 4, D))
    a["rms_w"] = i["L1_attn_rms_w"].reshape(KD, P).T
    freq = 1.0 / np.float32(10000.0) ** (np.arange(0, 64, 2, dtype=np.float32) / np.float32(64))
    ang = np.arange(T, dtype=np.float32)[None, :] * freq[:, None]
    co, si = np.cos(ang), np.sin(ang)
    a["rotary"] = np.stack([np.tile(co, (4, 1)), np.concatenate([-si, si, -si, si])], axis=1)
    two = lambda x: [x[:INNER], x[INNER:]]
    gate = np.stack(two(i["L0_ffn_shared_gate_w"]) + list(i["L0_ffn_gate_proj"]))
    up = np.stack(two(i["L0_ffn_shared_up_w"]) + list(i["L0_ffn_up_proj"]))
    gu = np.concatenate([gate, up], axis=1).transpose(0, 2, 1)
    a["f0_up"] = c(gu.reshape(18, KD, P, 2 * INNER).transpose(0, 2, 1, 3))
    down = np.stack(two(i["L0_ffn_shared_down_w"].T) + [x.T for x in i["L0_ffn_down_proj"]])
    a["f0_down"] = c(down)
    a["f0_router"] = c(i["L0_ffn_gate_weight"].T)
    a["f0_bias"] = i["L0_ffn_e_score_correction_bias"]
    w1 = np.stack([i["L1_ffn_w_shared1"]] + list(i["L1_ffn_w1"]))
    a["f1_up"] = c(w1.reshape(9, KD, P, INNER).transpose(0, 2, 1, 3))
    a["f1_down"] = c(np.stack([i["L1_ffn_w_shared2"]] + list(i["L1_ffn_w2"])))
    a["f1_router"] = i["L1_ffn_w_router"]
    for x in "qkvo":
        a[f"l_{x}"] = c(i[f"L1_xattn_W{x}"].T)
        a[f"l_b{x}"] = i[f"L1_xattn_b{x}"]
    for x in "qk":
        a[f"l_{x}f"] = c(i[f"L1_xattn_W{x}f"].T)
    for x in "qk":
        a[f"l_b{x}"] = a[f"l_b{x}"].reshape(KD, P).T
    a["l_mask"] = i["mask_BxS2_ff1"].reshape(B, CT, P).transpose(0, 2, 1)
    return {n: c(x) for n, x in a.items()}


def kernel(**inputs):
    import numpy as np
    import concourse.bacc as bacc
    from concourse.bass_utils import run_bass_kernel_spmd

    nc = bacc.Bacc("TRN2", target_bir_lowering=False, num_devices=1)
    arrays = _laid_out({n: np.asarray(x) for n, x in inputs.items()})
    t = {n: nc.dram_tensor(n, x.shape, mybir.dt.from_np(x.dtype), kind="ExternalInput").ap()
         for n, x in arrays.items()}
    t["out"] = nc.dram_tensor("out", _OUT[0][0], F32, kind="ExternalOutput").ap()
    program(nc, t)
    r = run_bass_kernel_spmd(nc, [arrays], core_ids=[0])
    return r.results[0]["out"]
```

```python
from contextlib import ExitStack

import concourse.bass as bass
from concourse import mybir

F32 = mybir.dt.float32
F32R = mybir.dt.float32r
BF16 = mybir.dt.bfloat16
U8 = mybir.dt.uint8
ALU = mybir.AluOpType
ACT = mybir.ActivationFunctionType
AX = mybir.AxisListType

P = 128
B, T, D = 2, 512, 512
NTOK = B * T
NT = NTOK // P
TT = T // P
KD = D // P
SC = 1024
CT = SC // P
INNER = 352
ITILES = [(0, 128), (128, 128), (256, 96)]
LN_EPS, RMS_EPS = 1e-5, 1e-6
MASKED = -1e30
SEM_START = 16384


class Mark:

    def __init__(self, sem, value, loop, back=0):
        self.sem, self.value, self.loop, self.back = sem, value, loop, back


class Loop:
    def __init__(self, n, start):
        self.n, self.start, self.per, self.index, self.over = n, start, {}, None, False


class Queue:

    ENGINES = ("pe", "act", "dve", "pool")

    def __init__(self, nc, sems):
        self.nc, self.sems = nc, sems
        self.engines = {"pe": nc.tensor, "act": nc.scalar, "dve": nc.vector, "pool": nc.gpsimd,
                        "sp": nc.sync}
        self.count = {s: 0 for s in sems}
        self.notes = {}
        self.loop_ = None
        self.dry = False
        self.seen = {e: {} for e in self.engines}
        for s in self.ENGINES:
            nc.sync.sem_inc(sems[s], SEM_START)
            self.count[s] = SEM_START

    def note(self, key, *marks):
        self.notes[key] = tuple(marks)

    def at(self, key):
        return self.notes.get(key, ())

    def _value(self, m):
        if m.loop is None:
            return m.value, None
        lp = m.loop
        if lp.over or m.back and lp is not self.loop_:
            return lp.start[m.sem] + (lp.n - 1) * lp.per.get(m.sem, 0) + m.value, None
        return lp.start[m.sem] + m.value - m.back * lp.per.get(m.sem, 0), lp

    def wait(self, eng, *marks):
        if self.dry:
            return
        most = {}
        for m in marks:
            v, lp = self._value(m)
            key = (m.sem, lp)
            most[key] = max(most.get(key, 0), v)
        for (s, lp), v in most.items():
            if self.seen[eng].get((s, lp), -1) >= v:
                continue
            self.seen[eng][(s, lp)] = v
            per = lp.per.get(s, 0) if lp else 0
            assert v > 0, (s, v)
            self.engines[eng].wait_ge(self.sems[s], lp.index * per + v if per else v)
            if per and eng in ("sp", "pool"):
                self.engines[eng].sem_inc(self.sems["passed"], 1)

    def op(self, eng, make, *waits, sem=None, by=1):
        sem = sem or eng
        if not self.dry:
            self.wait(eng, *waits)
            make(self.engines[eng]).then_inc(self.sems[sem], by)
        self.count[sem] += by
        base = self.loop_.start[sem] if self.loop_ else 0
        return Mark(sem, self.count[sem] - base, self.loop_)

    def quiet(self, eng, make, *waits):
        if not self.dry:
            self.wait(eng, *waits)
            make(self.engines[eng])

    def load(self, sem, make, *waits):
        return self.op("sp", make, *waits, sem=sem, by=16)

    def loop(self, n, body):
        lp = Loop(n, dict(self.count))
        before = dict(self.notes)
        self.loop_, self.dry = lp, True
        body(0)
        lp.per = {s: self.count[s] - lp.start[s] for s in self.count}
        ended = self.notes
        self.count = dict(lp.start)
        self.dry = False
        self.notes = dict(before)
        for k, marks in ended.items():
            back = tuple(Mark(m.sem, m.value, lp, 1) for m in marks if m.loop is lp)
            if back:
                self.notes[k] = before.get(k, ()) + back
        with self.nc.Fori(0, n) as i:
            lp.index = i
            body(i)
        assert all(self.count[s] - lp.start[s] == lp.per[s] for s in self.count)
        lp.over, self.loop_ = True, None
        self.count = {s: lp.start[s] + n * lp.per[s] for s in self.count}
        for seen in self.seen.values():
            for s, of in list(seen):
                if of is lp:
                    del seen[(s, of)]

    def fence(self):
        self.wait("sp", *[Mark(s, v, None) for s, v in self.count.items() if v and s != "fence"])
        told = self.op("sp", lambda e: e.nop(), sem="fence")
        for e in self.engines:
            if e != "sp":
                self.wait(e, told)
        self.notes = {}


def program(nc, t):
    ctx = ExitStack()
    with ctx:
        sems = {s: ctx.enter_context(nc.semaphore(f"s_{s}")) for s in
                ("pe", "act", "dve", "pool", "x", "small", "w", "w2", "ctx", "out", "turn0", "turn1", "fence", "passed")}
        q = Queue(nc, sems)
        bank = [ctx.enter_context(nc.psum_tensor(f"bank{i}", [P, 512], F32)) for i in range(8)]

        def sb(name, shape, dt=F32, scope=ctx):
            return scope.enter_context(nc.sbuf_tensor(name, [P] + list(shape), dt))

        X = sb("X", [NT, D])
        YH, YL = sb("YH", [KD, NTOK], F32R), sb("YL", [KD, NTOK], F32R)
        ident = sb("ident", [P])
        identb = sb("identb", [P], BF16)
        causal = sb("causal", [P], BF16)
        k = dict(q=q, bank=bank, sb=sb, X=X, YH=YH, YL=YL, ident=ident, identb=identb,
                 causal=causal, nc=nc)

        parts = [q.load(sem, lambda e: e.dma_start(
            X[:, 2 * i:2 * i + 2, :], t["x"].rearrange("b (t p) d -> p (b t) d", p=P)[:, 2 * i:2 * i + 2, :]))
                 for i, sem in enumerate(("x", "ctx", "turn0", "turn1"))]
        for i, part in enumerate(parts):
            q.note(f"x{i} loaded", part)
        q.note("x", *parts)
        zero = q.op("pool", lambda e: e.memset(ident[:, :], 0.0))
        zero2 = q.op("pool", lambda e: e.memset(causal[:, :], 0.0))
        m1 = q.op("pool", lambda e: e.affine_select(
            out=ident[:, :], in_=ident[:, :], compare_op=ALU.not_equal, fill=1.0, base=0,
            pattern=[[-1, P]], channel_multiplier=1), zero)
        m2 = q.op("pool", lambda e: e.affine_select(
            out=causal[:, :], in_=causal[:, :], compare_op=ALU.is_ge, fill=MASKED, base=0,
            pattern=[[-1, P]], channel_multiplier=1), zero2)
        m3 = q.op("dve", lambda e: e.tensor_copy(identb[:, :], ident[:, :]), m1)
        q.wait("pe", m1, m2, m3)

        attention(k, "a0", t["a0_qkv"], t["a0_wo"], heads=4, qtiles=1, hd=32)
        memory_attention(k, t["ctxT"], t["ctx"], t["mem_mask"])
        experts(k, "f0", t["f0_up"], t["f0_down"], routed=16, shared=2, gated=True,
                router=t["f0_router"], bias=t["f0_bias"])
        attention(k, "a1", t["a1_qkv"], t["a1_wo"], heads=2, qtiles=4, hd=64, rotary=t["rotary"],
                  rms=t["rms_w"])
        linear_attention(k, t)
        experts(k, "f1", t["f1_up"], t["f1_down"], routed=8, shared=1, gated=False,
                router=t["f1_router"], bias=None)
        end = q.load("out", lambda e: e.dma_start(
            t["out"].rearrange("b (t p) d -> p (b t) d", p=P), X[:, :, :]), *q.at("x"))
        q.wait("sp", end)
        q.fence()


def split(q, eng, hi, lo, src, *waits, scale=None, bias=None):
    hi32 = hi.bitcast(F32)
    if bias is not None:
        m = q.op("act", lambda e: e.activation(hi, src, ACT.Identity, bias=bias), *waits)
        return q.op(eng, lambda e: e.scalar_tensor_tensor(
            out=lo, in0=src, scalar=bias, in1=hi32, op0=ALU.add, op1=ALU.subtract), m)
    if scale is not None:
        m = q.op("act", lambda e: e.activation(hi, src, ACT.Copy, scale=scale), *waits)
        return q.op(eng, lambda e: e.scalar_tensor_tensor(
            out=lo, in0=src, scalar=scale, in1=hi32, op0=ALU.mult, op1=ALU.subtract), m)
    m = q.op("act", lambda e: e.activation(hi, src, ACT.Copy), *waits)
    return q.op(eng, lambda e: e.tensor_tensor(lo, src, hi32, ALU.subtract), m)


def splits(q, eng, parts, *waits, scale=1.0):
    for hi, _, src in parts:
        m = q.op("act", lambda e: e.activation(hi, src, ACT.Copy, scale=scale), *waits)
    for hi, lo, src in parts:
        last = q.op(eng, lambda e: e.scalar_tensor_tensor(
            out=lo, in0=src, scalar=scale, in1=hi.bitcast(F32), op0=ALU.mult, op1=ALU.subtract), m)
    return last


def product(q, out, lhs, rhs, *waits, first=True, last=True, check=True):
    n = len(lhs)
    m = None
    for i, ((lh, ll), (rh, rl)) in enumerate(zip(lhs, rhs)):
        for j, (a, b) in enumerate(((lh, rh), (lh, rl), (ll, rh))):
            make = lambda e: e.matmul(out, a, b, start=first and i == 0 and j == 0,
                                      stop=last and i == n - 1 and j == 2,
                                      skip_group_check=not check)
            if i == n - 1 and j == 2:
                m = q.op("pe", make, *waits)
            else:
                q.quiet("pe", make, *waits)
            waits = ()
    return m


class NormBuffers:

    def __init__(self, k, scope, name, n, y=None, rms=False):
        sb = lambda nm, shape: k["sb"](f"{name}_{nm}", shape, F32, scope)
        self.stats, self.moments, self.var = sb("stats", [n, 6]), sb("moments", [n, 2]), sb("var", [n])
        self.root, self.inv, self.u = sb("root", [n]), sb("inv", [n]), sb("u", [n])
        self.y = [sb(f"y{i}", [D])[:, :] for i in range(min(n, 4))] if y is None else y
        if rms:
            self.w, self.ln, self.shift = sb("w", [KD]), sb("ln", [n]), sb("shift", [n])


def inverse_root(q, f, *waits):
    v, r, u = f.var[:, :], f.inv[:, :], f.u[:, :]
    m = q.op("act", lambda e: e.activation(f.root[:, :], v, ACT.Sqrt), *waits)
    m = q.op("dve", lambda e: e.reciprocal(r, f.root[:, :]), m)
    m = q.op("dve", lambda e: e.tensor_tensor(u, r, r, ALU.mult), m)
    m = q.op("dve", lambda e: e.tensor_tensor(u, u, v, ALU.mult), m)
    m = q.op("dve", lambda e: e.tensor_scalar(u, u, -0.5, 1.5, ALU.mult, ALU.add), m)
    return q.op("dve", lambda e: e.tensor_tensor(r, r, u, ALU.mult), m)


def norm(k, f, n, x, yh, yl, rms=None, meanwhile=lambda: None):
    q, bank, ident = k["q"], k["bank"], k["ident"]

    def stats(of, *waits):
        ms = [q.op("dve", lambda e: e.bn_stats(f.stats[:, i, :], of(i)), *waits,
                   *(q.at(f"x{i // 2} loaded") or q.at("x"))) for i in range(n)]
        even, odd = f.stats[:, :, 1:3], f.stats[:, :, 4:6]
        dif, mean, var = f.u[:, :], f.moments[:, :, 0], f.moments[:, :, 1]
        m = q.op("dve", lambda e: e.tensor_tensor(f.moments[:, :, :], even, odd, ALU.add), ms[-1])
        d = q.op("dve", lambda e: e.tensor_tensor(dif, even[:, :, 0], odd[:, :, 0], ALU.subtract))
        v = q.op("dve", lambda e: e.tensor_scalar(var, var, 1.0 / D, None, ALU.mult), m)
        d = q.op("dve", lambda e: e.tensor_tensor(dif, dif, dif, ALU.mult), d)
        q.op("dve", lambda e: e.tensor_scalar(mean, mean, 0.5, None, ALU.mult))
        return q.op("dve", lambda e: e.scalar_tensor_tensor(
            out=var, in0=dif, scalar=0.25, in1=var, op0=ALU.mult, op1=ALU.add), d, v)

    m = stats(x, *q.at("y read"))
    m = q.op("dve", lambda e: e.tensor_scalar(f.var[:, :], f.moments[:, :, 1], LN_EPS, None,
                                              ALU.add), m)
    m = inverse_root(q, f, m)
    if rms is not None:
        got = q.load("small", lambda e: e.dma_start(f.w[:, :], rms))
        ln = q.op("dve", lambda e: e.tensor_copy(f.ln[:, :], f.inv[:, :]), m)
        m = q.op("dve", lambda e: e.tensor_tensor(f.var[:, :], f.moments[:, :, 1], f.inv[:, :], ALU.mult), m)
        m = q.op("dve", lambda e: e.tensor_tensor(f.var[:, :], f.var[:, :], f.inv[:, :], ALU.mult), m)
        m = q.op("dve", lambda e: e.tensor_scalar(f.var[:, :], f.var[:, :], RMS_EPS, None, ALU.add), m)
        m = inverse_root(q, f, m)
        m = q.op("dve", lambda e: e.tensor_tensor(f.inv[:, :], f.inv[:, :], f.ln[:, :], ALU.mult), m)
        neg = q.op("dve", lambda e: e.scalar_tensor_tensor(
            out=f.shift[:, :], in0=f.moments[:, :, 0], scalar=-1.0, in1=f.ln[:, :], op0=ALU.mult, op1=ALU.mult))
        shifted = q.op("dve", lambda e: e.tensor_scalar(f.ln[:, :], f.ln[:, :], 1.0, None, ALU.add), m, neg)
        q.wait("act", got)
        q.wait("dve", got)
    slots = len(f.y)
    ys = []

    def centre(i):
        ys.append(q.op("dve", lambda e: e.tensor_scalar(f.y[i % slots], x(i), f.moments[:, i, 0:1],
                                                        f.inv[:, i:i + 1], ALU.subtract, ALU.mult),
                       m_inv, *q.at(f"ny{i % slots} read")))

    m_inv = m
    for i in range(min(n, slots)):
        centre(i)
    meanwhile()
    last = None
    for i in range(n):
        b = i % 4
        for c in range(KD):
            m = q.op("pe", lambda e: e.transpose(bank[b][:, c * P:(c + 1) * P],
                                                 f.y[i % slots][:, c * P:(c + 1) * P], ident[:, :]),
                     ys[i], *q.at(f"bank{b} read"))
        q.note(f"ny{i % slots} read", m)
        ts = slice(i * P, i * P + P)
        src = bank[b][:, :].rearrange("p (c t) -> p c t", c=KD)
        if rms is None:
            last = split(q, "dve", yh[:, :, ts], yl[:, :, ts], src, m, *q.at("y read"))
        else:
            for c in range(KD):
                m = q.op("act", lambda e: e.activation(yh[:, c, ts], src[:, c, :], ACT.Copy,
                                                       scale=f.w[:, c:c + 1]), m)
            for c in range(KD):
                last = q.op("dve", lambda e: e.scalar_tensor_tensor(
                    out=yl[:, c, ts], in0=src[:, c, :], scalar=f.w[:, c:c + 1],
                    in1=yh[:, c, ts].bitcast(F32), op0=ALU.mult, op1=ALU.subtract), m)
        q.note(f"bank{b} read", last)
        if i + slots < n:
            centre(i + slots)
    q.note("y", last)
    if rms is not None:
        for i in range(n):
            m = q.op("pool", lambda e: e.tensor_scalar(x(i), x(i), f.ln[:, i:i + 1], f.shift[:, i:i + 1],
                                                       ALU.mult, ALU.add), shifted, ys[i])
        q.note("x", m)


def attention(k, name, w_qkv, w_out, heads, qtiles, hd, rotary=None, rms=None):
    q, bank, X, YH, YL = k["q"], k["bank"], k["X"], k["YH"], k["YL"]
    ident, identb, causal = k["ident"], k["identb"], k["causal"]
    scale = float(hd) ** -0.5
    steps = D // P if qtiles == 1 else 4
    s = ExitStack()
    sb = lambda nm, shape, dt=F32: k["sb"](f"{name}_{nm}", shape, dt, s)
    cols = (qtiles + 2) * P
    raw = sb("raw", [KD, max(cols, 512)])
    WH, WL = sb("WH", [qtiles + 3, KD, P], F32R), sb("WL", [qtiles + 3, KD, P], F32R)
    o_tile = lambda r: qtiles + 2 if r == 0 else r - 1
    QH, QL = sb("QH", [qtiles, NTOK], F32R), sb("QL", [qtiles, NTOK], F32R)
    KH, KL = sb("KH", [heads, NTOK], F32R), sb("KL", [heads, NTOK], F32R)
    VH, VL = sb("VH", [heads, NT, P], F32R), sb("VL", [heads, NT, P], F32R)
    SLOTS = 3
    E = [sb(f"E{i}", [1280]) for i in range(SLOTS)]
    PHL = sb("PHL", [4, 1280], F32R)
    PH, PL = [PHL[:, i, :] for i in range(2)], [PHL[:, 2 + i, :] for i in range(2)]
    top, total, inv = sb("top", [SLOTS, 4]), sb("total", [SLOTS, 4]), sb("inv", [SLOTS, 4])
    if rotary is not None:
        swapped = [sb(f"swapped{i}", [NTOK]) for i in range(2)]
        cos_sin = sb("cos_sin", [2, T])
        q.load("small", lambda e: e.dma_start(cos_sin[:, :, :], rotary))
    for z in (KH, KL):
        m = q.op("pool", lambda e: e.memset(z[:, :, :].bitcast(F32), 0.0))
    q.note("K read", m)
    for z in (VH, VL):
        m = q.op("pool", lambda e: e.memset(z[:, :, :, :].bitcast(F32), 0.0))
    q.note("V read", m)
    f = NormBuffers(k, s, f"{name}_n", NT, [E[i][:, a * D:(a + 1) * D] for i in range(SLOTS) for a in range(2)],
                    rms is not None)
    norm(k, f, NT, lambda i: X[:, i, :], YH, YL, rms)
    ym = q.at("y")
    for i in range(SLOTS):
        q.note(f"E{i} read", *ym)
    e_at = [0, 128, 384, 768]
    chunks = [[(3, 0)], [(2, 0), (0, 384)], [(1, 0)]]
    p_at = [0, 512, 1024, 896]
    tchunks = [[(0, 0)], [(1, 0), (3, 384)], [(2, 0)]]
    p_chunk = [(0, 512), (512, 512), (1024, 256)]
    SR, TR, OB = 4, 3, 7

    head_rows = [(h, slice(h * hd, h * hd + hd)) for h in range(heads)]
    queries = [qtiles - 1] + list(range(qtiles - 1))
    order = [qtiles] + queries
    slot = lambda c: order.index(c) % 2

    def body(j):
        w_in = q.load("w", lambda e: e.dma_start(raw[:, :, 0:cols], w_qkv[j]), *q.at("raw read"))
        ready = {}
        for c in order + [qtiles + 1]:
            a = slice(c * P, c * P + P)
            ready[c] = split(q, "pool", WH[:, c, :, :], WL[:, c, :, :], raw[:, :, a], w_in,
                             *q.at(f"W{c} read"))
        q.note("raw read", ready[qtiles + 1])
        w = lambda c, kk: (WH[:, c, kk, :], WL[:, c, kk, :])
        y = lambda kk, a: (YH[:, kk, a], YL[:, kk, a])
        n = 0
        done = {}

        def rotate(c):
            f, o, rot = E[slot(c)], swapped[slot(c)], E[2]
            half = [slice(b * T, b * T + T) for b in range(B)]
            for a in half:
                p2 = q.op("pool", lambda e: e.tensor_tensor(o[:, a], o[:, a], cos_sin[:, 1, :],
                                                            ALU.mult), turned[c])
                p1 = q.op("dve", lambda e: e.tensor_tensor(rot[:, a], f[:, a], cos_sin[:, 0, :],
                                                           ALU.mult), turned[c], *q.at("E2 read"))
            p3 = q.op("dve", lambda e: e.tensor_tensor(rot[:, 0:NTOK], rot[:, 0:NTOK], o[:, :], ALU.add),
                      p1, p2)
            z = (order.index(c) + 1) % 2
            to = [(PH[z][:, 0:NTOK], PL[z][:, 0:NTOK], slice(0, P))] if c < qtiles else [
                (KH[ps, h, :], KL[ps, h, :], ps) for h, ps in head_rows]
            by = scale if c < qtiles else 1.0
            free = q.at(f"P{z} read") + q.at(f"Q{c} read") if c < qtiles else q.at("K read")
            his = [(a, hi, lo, ps, q.op("act", lambda e: e.activation(
                hi[:, a], rot[ps, a], ACT.Copy, scale=by), p3, *free)) for a in half for hi, lo, ps in to]
            for a, hi, lo, ps, m in his:
                m = q.op("dve", lambda e: e.scalar_tensor_tensor(
                    out=lo[:, a], in0=rot[ps, a], scalar=by, in1=hi[:, a].bitcast(F32), op0=ALU.mult,
                    op1=ALU.subtract), m)
            up, dn = slice(0, hd), slice(hd, P)
            moves = ([(QH[up, c, :], PH[z][up, 0:NTOK]), (QH[dn, c, :], PL[z][up, 0:NTOK]),
                      (QL[up, c, :], PL[z][dn, 0:NTOK]), (QL[dn, c, :], PH[z][dn, 0:NTOK])] if c < qtiles else
                     [(KH[dn, 0, :], KH[up, 0, :]), (KH[up, 1, :], KH[dn, 1, :])])
            for out_, in_ in moves:
                stacked = q.load(("ctx", "x")[slot(c)], lambda e: e.dma_start(
                    out_.bitcast(F32), in_.bitcast(F32)), m)
            if c < qtiles:
                q.note(f"P{z} read", stacked)
            done[c, 0] = done[c, 1] = stacked
            q.note(f"E{slot(c)} read", p1)
            q.note("E2 read", m)
            q.note(f"swapped{slot(c)} read", p3)

        turned = {}

        def projected(c, b):
            nonlocal n
            bk, n = n % 8, n + 1
            a = slice(b * T, b * T + T)
            m = product(q, bank[bk][:, :], [w(c, kk) for kk in range(KD)], [y(kk, a) for kk in range(KD)],
                        ready[c], *ym, *q.at(f"bank{bk} read"))
            q.note(f"W{c} read", m)
            return bk, m

        def tile(c):
            for b in range(B):
                bk, m = projected(c, b)
                a = slice(b * T, b * T + T)
                if c < qtiles:
                    done[c, b] = split(q, "dve", QH[:, c, a], QL[:, c, a], bank[bk][:, :], m,
                                       *q.at(f"Q{c} read"), scale=scale)
                else:
                    done[c, b] = splits(q, "dve", [(KH[ps, h, a], KL[ps, h, a], bank[bk][ps, :])
                                                   for h, ps in head_rows], m, *q.at("K read"))
                q.note(f"bank{bk} read", done[c, b])

        def tile_to_rotate(c):
            f = E[slot(c)]
            for b in range(B):
                bk, m = projected(c, b)
                m = q.op("act", lambda e: e.activation(f[:, b * T:b * T + T], bank[bk][:, :], ACT.Copy), m,
                         *q.at(f"E{slot(c)} read"))
                q.note(f"bank{bk} read", m)
            for x in range(4):
                turned[c] = q.load(f"turn{slot(c)}", lambda e: e.dma_start(
                    swapped[slot(c)][32 * x:32 * x + 32, :], f[32 * (x ^ 1):32 * (x ^ 1) + 32, 0:NTOK]),
                    m, *q.at(f"swapped{slot(c)} read"))

        def value_tile():
            for b in range(B):
                bk, m = projected(qtiles + 1, b)
                evac[b] = q.op("act", lambda e: e.activation(E[1][:, b * T:b * T + T], bank[bk][:, :], ACT.Copy),
                               m, *q.at("E1 read"))
                q.note(f"bank{bk} read", evac[b])

        def values_of(b):
            nonlocal n
            bk, n = n % 8, n + 1
            for i in range(TT):
                m = q.op("pe", lambda e: e.transpose(bank[bk][:, i * P:(i + 1) * P],
                                                     E[1][:, b * T + i * P:b * T + (i + 1) * P], ident[:, :]),
                         evac[b], *q.at(f"bank{bk} read"))
            src = bank[bk][:, :].rearrange("p (i c) -> p i c", i=TT)
            bs = slice(b * TT, b * TT + TT)
            done["v", b] = splits(q, "dve", [(VH[:, h, bs, cs], VL[:, h, bs, cs], src[:, :, cs])
                                             for h, cs in head_rows], m, *q.at("V read"))
            q.note(f"bank{bk} read", done["v", b])
            if b == B - 1:
                q.note("E1 read", m)

        evac = {}
        if rotary is None:
            for c in order:
                tile(c)
        else:
            for x, c in enumerate(order):
                tile_to_rotate(c)
                if x >= 1:
                    rotate(order[x - 1])
        value_tile()
        for b in range(B):
            values_of(b)
        wo_in = q.load("w2", lambda e: e.dma_start(raw[:, 0:qtiles, 0:D], w_out[j]), *q.at("raw read"))

        jobs = [(b, r, h) for b in range(B) for r in queries for h in range(heads)]
        S, MX, EX, NRM, TP, OUT, sbank = {}, {}, {}, {}, {}, {}, {}
        taken, wo = 0, []

        def ring():
            nonlocal taken
            taken += 1
            return (taken - 1) % SR

        o = lambda x, r: x[:, o_tile(r), :, :].rearrange("p k n -> p (k n)")

        def output_weights(r):
            wo.append(split(q, "pool", o(WH, r), o(WL, r), raw[:, r, 0:D], wo_in,
                            *q.at(f"W{o_tile(r)} read")))
            q.note("raw read", *wo)

        def output(g):
            bk = ring()
            a = slice(g * P, g * P + P)
            m = product(q, bank[bk][:, :], [(QH[:, r, a], QL[:, r, a]) for r in range(qtiles)],
                        [(o(WH, r), o(WL, r)) for r in range(qtiles)], *wo,
                        *[OUT[r, g // TT] for r in range(qtiles)], *q.at(f"bank{bk} read"))
            add = q.op("dve", lambda e: e.tensor_tensor(X[:, g, :], bank[bk][:, :], X[:, g, :],
                                                        ALU.add), m, *q.at("x"))
            q.note(f"bank{bk} read", add)
            return m, add

        def scores(n):
            b, r, h = jobs[n]
            for ci, chunk in enumerate(chunks):
                bk = sbank[n, ci] = ring()
                for i, off in chunk:
                    w_ = P * (i + 1)
                    qs = slice(b * T + i * P, b * T + i * P + P)
                    ks = slice(b * T, b * T + w_)
                    if rotary is None:
                        product(q, bank[bk][:, off:off + w_], [(QH[:, r, qs], QL[:, r, qs])],
                                [(KH[:, h, ks], KL[:, h, ks])], done[r, b], done[qtiles, b],
                                *q.at(f"bank{bk} read"), last=False)
                    else:
                        for x, keys in enumerate((KH, KL)):
                            q.quiet("pe", lambda e: e.matmul(
                                bank[bk][:, off:off + w_], (QH, QL)[h][:, r, qs], keys[:, h, ks], start=x == 0,
                                stop=False), done[r, b], done[qtiles, b], *q.at(f"bank{bk} read"))
                    S[n, ci] = q.op("pe", lambda e: e.matmul(
                        bank[bk][:, off + i * P:off + w_], identb[:, :], causal[:, :],
                        start=False, stop=True))

        def maxima(n):
            sl = (n + 1) % SLOTS
            for ci, chunk in enumerate(chunks):
                for i, off in chunk:
                    MX[n, i] = q.op("dve", lambda e: e.tensor_reduce(
                        top[:, sl, i:i + 1], bank[sbank[n, ci]][:, off:off + P * (i + 1)], AX.X, ALU.max,
                        negate=True), S[n, ci], *EX.get(n - SLOTS, ()))

        def exponentials(n):
            sl = (n + 1) % SLOTS
            for ci, chunk in enumerate(chunks):
                bk = sbank[n, ci]
                for i, off in chunk:
                    m = q.op("act", lambda e: e.activation(
                        E[sl][:, e_at[i]:e_at[i] + P * (i + 1)], bank[bk][:, off:off + P * (i + 1)],
                        ACT.Exp, bias=top[:, sl, i:i + 1], accum_out=total[:, sl, i:i + 1]),
                        MX[n, i], MX[n, chunk[-1][0]], *(q.at(f"E{sl} read")))
                q.note(f"bank{bk} read", m)
            EX[n] = (m,)

        def normalise(n):
            sl = (n + 1) % SLOTS
            m = q.op("dve", lambda e: e.reciprocal(inv[:, sl, :], total[:, sl, :]), *EX[n],
                     *NRM.get((n - SLOTS, 3), ()), *q.at(f"inv{sl} read"))
            for i in range(TT):
                a = slice(e_at[i], e_at[i] + P * (i + 1))
                NRM[n, i] = (q.op("pool", lambda e: e.tensor_scalar(
                    E[sl][:, a], E[sl][:, a], inv[:, sl, i:i + 1], 0.0, ALU.mult, ALU.add), m),)
            q.note(f"inv{sl} read", *NRM[n, 3])

        def transposes(n):
            sl = (n + 1) % SLOTS
            for ci, chunk in enumerate(tchunks):
                bk = SR + (3 * n + ci) % TR
                for sblk, off in chunk:
                    for i in range(sblk, TT):
                        at = off + (i - sblk) * P
                        m = q.op("pe", lambda e: e.transpose(
                            bank[bk][:, at:at + P],
                            E[sl][:, e_at[i] + sblk * P:e_at[i] + (sblk + 1) * P], ident[:, :]),
                            *NRM[n, i], *q.at(f"bank{bk} read"))
                at, size = p_chunk[ci]
                a = slice(at, at + size)
                TP[n, ci] = split(q, "dve", PH[n % 2][:, a], PL[n % 2][:, a], bank[bk][:, 0:size],
                                  m, *q.at(f"P{n % 2} read"))
                q.note(f"bank{bk} read", TP[n, ci])
            q.note(f"E{sl} read", m)

        def values(n):
            b, r, h = jobs[n]
            for ci, chunk in enumerate(tchunks):
                for sblk, _ in chunk:
                    w_ = T - sblk * P
                    a = slice(p_at[sblk], p_at[sblk] + w_)
                    v = (VH[:, h, b * TT + sblk, :], VL[:, h, b * TT + sblk, :])
                    m = product(q, bank[OB][:, sblk * P:T], [v], [(PH[n % 2][:, a], PL[n % 2][:, a])],
                                TP[n, ci], done["v", b], *(q.at("bank7 read") if h == 0 else ()),
                                first=h == 0 and sblk == 0, last=h == heads - 1 and ci == 2)
            q.note(f"P{n % 2} read", m)
            if h == heads - 1:
                a = slice(b * T, b * T + T)
                OUT[r, b] = split(q, "dve", QH[:, r, a], QL[:, r, a], bank[OB][:, :], m)
                q.note("bank7 read", OUT[r, b])

        J = len(jobs)
        between = {12: 0, 14: 1, 16: 2, 17: 3} if J == 16 else {7: 0, 8: 1, 9: 2, 10: 3}
        for n in range(J + 3):
            if n < J:
                scores(n)
                maxima(n)
            if n == 0 and rotary is not None:
                rotate(order[-1])
            if 2 <= n < 2 + qtiles:
                output_weights(n - 2)
            if 1 <= n <= J:
                normalise(n - 1)
            if 2 <= n < J + 2:
                transposes(n - 2)
            if n < J:
                exponentials(n)
            if n in between:
                output(between[n])
            if n >= 3:
                values(n - 3)
        q.note("K read", S[J - 1, 2])
        q.note("V read", *q.at(f"P{(J - 1) % 2} read"))
        for g in range(TT, NT):
            m, add = output(g)
        q.note("x", add)
        for r in range(qtiles):
            q.note(f"W{o_tile(r)} read", m)
            q.note(f"Q{r} read", m)

    q.loop(steps, body)
    q.fence()
    s.close()


def memory_attention(k, ctxT, ctx_rows, mask):
    q, bank, X, YH, YL = k["q"], k["bank"], k["X"], k["YH"], k["YL"]
    ident = k["ident"]
    scale = float(D) ** -0.5
    s = ExitStack()
    sb = lambda nm, shape, dt=F32: k["sb"](f"m_{nm}", shape, dt, s)
    half = CT // 2
    craw, rraw = sb("craw", [KD, SC]), sb("rraw", [CT, D])
    CH, CL = sb("CH", [KD, SC], F32R), sb("CL", [KD, SC], F32R)
    RH, RL = sb("RH", [CT, D], F32R), sb("RL", [CT, D], F32R)
    ma, mf = sb("ma", [B, SC], U8), sb("mf", [SC])
    mb, valid = sb("mb", [B, SC], BF16), sb("valid", [B])
    ones = sb("ones", [P], BF16)
    E = [sb(f"E{i}", [SC]) for i in range(2)]
    PH, PL = [sb(f"PH{i}", [SC], F32R) for i in range(2)], [sb(f"PL{i}", [SC], F32R) for i in range(2)]
    top, total = sb("top", [NT, 2]), sb("total", [NT, 2])
    nb, inv = sb("nb", [NT]), sb("inv", [NT])
    m_in = [q.load("small", lambda e: e.dma_start(
        ma[:, b, :], mask[b].rearrange("(a n) -> a n", a=1).broadcast_to([P, SC]))) for b in range(B)][-1]
    z = q.op("pool", lambda e: e.memset(ones[:, :], 0.0))
    z = q.op("pool", lambda e: e.memset(ones[0:1, :], 1.0), z)
    mm, vm, cm, rm = {}, {}, {}, {}

    def load_context(b):
        cl = [q.load(sem, lambda e: e.dma_start(craw[:, a, :], ctxT[b, :, a, :]), *q.at("craw read"))
              for sem, a in (("ctx", slice(0, 2)), ("w", slice(2, 4)))]
        rl = q.load("w2", lambda e: e.dma_start(rraw[:, :, :], ctx_rows[b]), *q.at("rraw read"))
        return cl, rl

    def masks(b):
        m = q.op("pool", lambda e: e.tensor_copy(mf[:, :], ma[:, b, :]), m_in, *q.at("mf read"))
        mm[b] = q.op("pool", lambda e: e.tensor_scalar(mb[:, b, :], mf[:, :], -MASKED, MASKED, ALU.mult,
                                                       ALU.add), m)
        return m

    def valid_(b, m):
        vm[b] = q.op("dve", lambda e: e.tensor_reduce(valid[:, b:b + 1], mf[:, :], AX.X, ALU.max), m)
        q.note("mf read", vm[b])

    def split_context(b, cl, engines):
        ms = []
        for kk in range(KD):
            ms.append(split(q, engines[kk], CH[:, kk, :], CL[:, kk, :], craw[:, kk, :], cl[kk // 2],
                            *q.at("C read")))
        q.note("craw read", *ms)
        cm[b] = ms

    def split_rows(b, rl):
        ms = [split(q, ("pool", "dve")[c % 2], RH[:, c, :], RL[:, c, :], rraw[:, c, :], rl, *q.at("R read"))
              for c in range(CT)]
        q.note("rraw read", *ms[-2:])
        rm[b] = ms[-2:]

    cl, rl = load_context(0)
    kept = masks(0)
    f = NormBuffers(k, s, "m_n", NT)
    split_context(0, cl, ["pool"] * KD)
    norm(k, f, NT, lambda i: X[:, i, :], YH, YL)
    ym = q.at("y")
    valid_(0, kept)
    EX, TP, IM = {}, {}, {}

    def scores(i):
        b = i // TT
        for h in range(2):
            bk = (2 * i + h) % 4
            a = slice(h * 512, h * 512 + 512)
            ts = slice(i * P, i * P + P)
            product(q, bank[bk][:, :], [(YH[:, kk, ts], YL[:, kk, ts]) for kk in range(KD)],
                    [(CH[:, kk, a], CL[:, kk, a]) for kk in range(KD)], *cm[b], *ym,
                    *q.at(f"bank{bk} read"), last=False)
            sm = q.op("pe", lambda e: e.matmul(bank[bk][:, :], ones[:, :], mb[:, b, a], start=False,
                                               stop=True), mm[b], z)
            m = q.op("dve", lambda e: e.tensor_reduce(top[:, i, h:h + 1], bank[bk][:, :], AX.X,
                                                      ALU.max), sm)
        m = q.op("dve", lambda e: e.tensor_reduce(nb[:, i:i + 1], top[:, i, :], AX.X, ALU.max,
                                                  negate=True), m)
        m = q.op("dve", lambda e: e.tensor_scalar(nb[:, i:i + 1], nb[:, i:i + 1], scale, None,
                                                  ALU.mult), m)
        for h in range(2):
            bk = (2 * i + h) % 4
            a = slice(h * 512, h * 512 + 512)
            EX[i] = q.op("act", lambda e: e.activation(
                E[i % 2][:, a], bank[bk][:, :], ACT.Exp, bias=nb[:, i:i + 1], scale=scale,
                accum_out=total[:, i, h:h + 1]), m, *q.at(f"mE{i % 2} read"))
            q.note(f"bank{bk} read", EX[i])
        q.note("C read", sm)

    def transposes(i):
        for h in range(2):
            bk = 4 + h
            for c in range(half):
                m = q.op("pe", lambda e: e.transpose(
                    bank[bk][:, c * P:(c + 1) * P],
                    E[i % 2][:, (h * half + c) * P:(h * half + c + 1) * P], ident[:, :]),
                    EX[i], *q.at(f"bank{bk} read"))
            a = slice(h * 512, h * 512 + 512)
            TP[i] = split(q, "dve", PH[i % 2][:, a], PL[i % 2][:, a], bank[bk][:, :], m,
                          *q.at(f"mP{i % 2} read"))
            q.note(f"bank{bk} read", TP[i])
        q.note(f"mE{i % 2} read", m)
        m = q.op("dve", lambda e: e.tensor_tensor(inv[:, i:i + 1], total[:, i, 0:1],
                                                  total[:, i, 1:2], ALU.add), EX[i])
        m = q.op("dve", lambda e: e.reciprocal(inv[:, i:i + 1], inv[:, i:i + 1]), m)
        IM[i] = q.op("dve", lambda e: e.tensor_tensor(inv[:, i:i + 1], inv[:, i:i + 1],
                                                      valid[:, i // TT:i // TT + 1], ALU.mult), m, vm[i // TT])

    def out(i):
        bk = 6 + i % 2
        m = product(q, bank[bk][:, :],
                    [(PH[i % 2][:, c * P:(c + 1) * P], PL[i % 2][:, c * P:(c + 1) * P])
                     for c in range(CT)],
                    [(RH[:, c, :], RL[:, c, :]) for c in range(CT)], TP[i], *rm[i // TT],
                    *q.at(f"bank{bk} read"))
        q.note(f"mP{i % 2} read", m)
        q.note("R read", m)
        add = q.op("dve", lambda e: e.scalar_tensor_tensor(
            out=X[:, i, :], in0=bank[bk][:, :], scalar=inv[:, i:i + 1], in1=X[:, i, :], op0=ALU.mult,
            op1=ALU.add), m, IM[i])
        q.note(f"bank{bk} read", add)
        q.note("x", add)

    for n in range(NT + 2):
        if n == 1:
            split_rows(0, rl)
            cl, rl = load_context(1)
            kept = masks(1)
        if n == 2:
            valid_(1, kept)
        if n == TT:
            split_context(1, cl, ["dve", "pool"] * 2)
        if n >= 2:
            out(n - 2)
        if 1 <= n <= NT:
            transposes(n - 1)
        if n == TT + 1:
            split_rows(1, rl)
        if n < NT:
            scores(n)
    q.fence()
    s.close()


def router_ranks(q, sb, name, v, shape, top, *waits):
    n = shape[-1]
    before, ge = sb(f"{name}_before", shape), [sb(f"{name}_ge{i}", shape) for i in range(2)]
    m = q.op("dve", lambda e: e.memset(before[:, :, :], 0.0), *waits)
    yield
    for d in range(1, n):
        g = ge[d % 2][:, :, 0:n - d]
        m1 = q.op("dve", lambda e: e.tensor_tensor(g, v[:, :, 0:n - d], v[:, :, d:n], ALU.is_ge), m)
        yield
        m2 = q.op("dve", lambda e: e.tensor_tensor(before[:, :, d:n], before[:, :, d:n], g, ALU.subtract), m1)
        yield
        m = q.op("dve", lambda e: e.scalar_tensor_tensor(
            out=before[:, :, 0:n - d], in0=g, scalar=1.0, in1=before[:, :, 0:n - d], op0=ALU.subtract,
            op1=ALU.add), m2)
        yield
    m = q.op("dve", lambda e: e.tensor_scalar(before[:, :, :], before[:, :, :], 0.5 - top, None,
                                              ALU.is_ge), m)
    yield
    return before, m


def experts(k, name, w_up, w_down, routed, shared, gated, router, bias):
    q, bank, X, YH, YL = k["q"], k["bank"], k["X"], k["YH"], k["YL"]
    s = ExitStack()
    sb = lambda nm, shape, dt=F32: k["sb"](f"{name}_{nm}", shape, dt, s)
    E_ = routed + shared
    cols = INNER * (2 if gated else 1)
    raw, UH, UL = sb("raw", [KD, cols]), sb("UH", [KD, cols], F32R), sb("UL", [KD, cols], F32R)
    draw = sb("draw", [3, D])
    DH, DL = sb("DH", [3, D], F32R), sb("DL", [3, D], F32R)
    HH, HL = sb("HH", [3, NTOK], F32R), sb("HL", [3, NTOK], F32R)
    act = [sb(f"act{i}", [512]) for i in range(2)]
    hid = [sb(f"hid{i}", [512]) for i in range(2)]
    comb, cw = sb("comb", [NT, E_ - 1]), sb("cw", [NT])
    f = NormBuffers(k, s, f"{name}_n", NT, [x[:, :] for x in act + hid])

    def up_weights(e_):
        up_in = q.load("w", lambda e: e.dma_start(raw[:, :, :], w_up[e_]), *q.at("raw read"))
        q.load("w2", lambda e: e.dma_start(
            draw[:, 0:2, :], w_down[e_, 0:256, :].rearrange("(k p) n -> p k n", p=P)), *q.at("draw read"))
        dn_in = q.load("w2", lambda e: e.dma_start(draw[0:96, 2, :], w_down[e_, 256:INNER, :]))
        if isinstance(e_, int):
            um = [split(q, ("pool", "dve")[kk % 2], UH[:, kk, :], UL[:, kk, :], raw[:, kk, :], up_in)
                  for kk in range(KD)]
        else:
            um = [split(q, "pool", UH[:, :, :], UL[:, :, :], raw[:, :, :], up_in, *q.at("U read"))]
        q.note("raw read", *um)
        return um, dn_in

    def down_weights(dn_in):
        split(q, "pool", DH[:, 0:2, :], DL[:, 0:2, :], draw[:, 0:2, :], dn_in, *q.at("D read"))
        dm = split(q, "pool", DH[0:96, 2, :], DL[0:96, 2, :], draw[0:96, 2, :], dn_in)
        q.note("draw read", dm)
        return dm

    first_up = []
    norm(k, f, NT, lambda i: X[:, i, :], YH, YL, meanwhile=lambda: first_up.append(up_weights(0)))
    ym = q.at("y")
    for x in ("act0", "act1", "hid0", "hid1"):
        q.note(f"{x} read", *ym)
    q.wait("pe", *ym)
    routing = route(k, sb, name, router, bias, routed, shared, comb)

    def body(e_, aside=lambda: None):
        um, dn_in = first_up[0] if isinstance(e_, int) else up_weights(e_)
        dm = down_weights(dn_in)
        first = isinstance(e_, int)
        if not first:
            cm = q.op("dve", lambda e: e.tensor_scalar(
                cw[:, :], comb[:, :, bass.ds(e_ - 1, 1)].rearrange("p t a -> p (t a)"), 1.0, None, ALU.mult),
                *q.at("x"))
        H = {}
        n = 0
        for b in range(B):
            ts = slice(b * T, b * T + T)
            y = [(YH[:, kk, ts], YL[:, kk, ts]) for kk in range(KD)]
            for it, (r0, rows) in enumerate(ITILES):
                gb, ub = (2 * n) % 4, (2 * n + 1) % 4
                sl = n % 2
                n += 1
                wt = lambda c: [(UH[:, kk, c:c + rows], UL[:, kk, c:c + rows]) for kk in range(KD)]
                gm = product(q, bank[gb][0:rows, :], wt(r0), y, *um, *q.at(f"bank{gb} read"))
                if gated:
                    pm = product(q, bank[ub][0:rows, :], wt(INNER + r0), y, *q.at(f"bank{ub} read"))
                else:
                    pm = gm
                am = q.op("act", lambda e: e.activation(act[sl][0:rows, :], bank[gb][0:rows, :],
                                                        ACT.Silu), gm, *q.at(f"act{sl} read"))
                q.note(f"bank{gb} read", am)
                src = act
                if gated:
                    am = q.op("dve", lambda e: e.tensor_tensor(
                        hid[sl][0:rows, :], bank[ub][0:rows, :], act[sl][0:rows, :], ALU.mult),
                        am, pm, *q.at(f"hid{sl} read"))
                    q.note(f"bank{ub} read", am)
                    q.note(f"act{sl} read", am)
                    src = hid
                H[it, b] = split(q, "dve", HH[0:rows, it, ts], HL[0:rows, it, ts],
                                 src[sl][0:rows, :], am, *q.at(f"H{b} read"))
                q.note(f"{'hid' if gated else 'act'}{sl} read", H[it, b])
                aside()
        q.note("U read", pm)
        for g in range(NT):
            bk = 4 + g % 4
            a = slice(g * P, g * P + P)
            m = product(q, bank[bk][:, :],
                        [(HH[0:rows, it, a], HL[0:rows, it, a]) for it, (_, rows) in enumerate(ITILES)],
                        [(DH[0:rows, it, :], DL[0:rows, it, :]) for it, (_, rows) in enumerate(ITILES)],
                        dm, *[H[it, g // TT] for it in range(3)], *q.at(f"bank{bk} read"))
            if first:
                add = q.op("dve", lambda e: e.tensor_tensor(X[:, g, :], bank[bk][:, :], X[:, g, :], ALU.add), m)
            else:
                add = q.op("dve", lambda e: e.scalar_tensor_tensor(
                    out=X[:, g, :], in0=bank[bk][:, :], scalar=cw[:, g:g + 1], in1=X[:, g, :],
                    op0=ALU.mult, op1=ALU.add), m, cm)
            aside()
            q.note(f"bank{bk} read", add)
            q.note(f"H{g // TT} read", m)
        q.note("D read", m)
        q.note("x", add)

    steps = iter([1, 1] + [12] * 4 + [6] * NT)
    body(0, lambda: [next(routing, None) for _ in range(next(steps))])
    for _ in routing:
        pass
    q.loop(E_ - 1, lambda i: body(i + 1) if not q.dry else body(Ellipsis))
    q.fence()
    s.close()


def route(k, sb, name, router, bias, routed, shared, comb):
    q, bank, YH, YL = k["q"], k["bank"], k["YH"], k["YL"]
    R = routed
    raw = sb("rw", [KD, R])
    RH, RL = sb("rh", [KD, R], F32R), sb("rl", [KD, R], F32R)
    lt = sb("lt", [NTOK])
    sc = sb("sc", [NT, R])
    den = sb("den", [NT])
    got = q.load("small", lambda e: e.dma_start(raw[:, :, :], router.rearrange("(k p) n -> p k n", p=P)))
    m = split(q, "dve", RH[:, :, :], RL[:, :, :], raw[:, :, :], got)
    for b in range(B):
        a = slice(b * T, b * T + T)
        lm = product(q, bank[4 + b][0:R, :], [(RH[:, kk, :], RL[:, kk, :]) for kk in range(KD)],
                     [(YH[:, kk, a], YL[:, kk, a]) for kk in range(KD)], m)
        m2 = q.op("act", lambda e: e.activation(lt[0:R, a], bank[4 + b][0:R, :], ACT.Copy), lm)
        q.note(f"bank{4 + b} read", m2)
    yield
    for g in range(NT):
        m = q.op("pe", lambda e: e.transpose(bank[6][:, g * R:(g + 1) * R], lt[0:R, g * P:(g + 1) * P],
                                             k["ident"][0:R, 0:R]), m2)
    logits = sb("lg", [NT, R])[:, :, :]
    m = q.op("dve", lambda e: e.tensor_copy(logits, bank[6][:, 0:NT * R].rearrange("p (t r) -> p t r", r=R)), m)
    q.note("bank6 read", m)
    yield
    if bias is not None:
        G, TOPG, TOPK, FACTOR = 4, 2, 6, 2.5
        S_ = R // G
        bs, ch = sb("bs", [R]), sb("ch", [NT, R])
        pair, gs, gt = sb("pair", [NT * G, 6]), sb("gs", [NT, G]), sb("gt", [NT * G, S_])
        bm = q.load("turn0", lambda e: e.dma_start(
            bs[:, :], bias.rearrange("(a n) -> a n", a=1).broadcast_to([P, R])))
        sm = q.op("act", lambda e: e.activation(sc[:, :, :], logits, ACT.Sigmoid), m)
        m = q.op("dve", lambda e: e.tensor_tensor(
            ch[:, :, :], sc[:, :, :], bs[:, :].rearrange("p (a r) -> p a r", a=1).broadcast_to([P, NT, R]),
            ALU.add), sm, bm)
        yield
        c4 = ch[:, :, :].rearrange("p t (g s) -> p (t g) s", g=G)
        at = 0
        for d in range(1, S_):
            pm = q.op("dve", lambda e: e.tensor_tensor(pair[:, :, at:at + S_ - d], c4[:, :, 0:S_ - d],
                                                       c4[:, :, d:S_], ALU.add), m)
            yield
            at += S_ - d
        gm = q.op("dve", lambda e: e.tensor_reduce(gs[:, :, :].rearrange("p t g -> p (t g)"),
                                                   pair[:, :, :], AX.X, ALU.max), pm)
        yield
        group, gm = yield from router_ranks(q, sb, f"{name}_g", gs, [NT, G], TOPG, gm)
        gf = group[:, :, :].rearrange("p t g -> p (t g)")
        tm = q.op("dve", lambda e: e.tensor_tensor(
            gt[:, :, :], c4, gf.rearrange("p (n a) -> p n a", a=1).broadcast_to([P, NT * G, S_]),
            ALU.mult), gm)
        yield
        chosen, m = yield from router_ranks(q, sb, f"{name}_e", gt[:, :, :].rearrange("p (t g) s -> p t (g s)", g=G),
                                 [NT, R], TOPK, tm)
    else:
        TOPK, FACTOR = 2, 1.0
        mx = sb("mx", [NT])
        bc = lambda a: a.rearrange("p (t a) -> p t a", a=1).broadcast_to([P, NT, R])
        m = q.op("dve", lambda e: e.tensor_reduce(mx[:, :], logits, AX.X, ALU.max), m)
        yield
        m = q.op("dve", lambda e: e.tensor_tensor(sc[:, :, :], logits, bc(mx[:, :]), ALU.subtract), m)
        yield
        m = q.op("act", lambda e: e.activation(sc[:, :, :], sc[:, :, :], ACT.Exp), m)
        m = q.op("dve", lambda e: e.tensor_reduce(den[:, :], sc[:, :, :], AX.X, ALU.add), m)
        yield
        m = q.op("dve", lambda e: e.reciprocal(den[:, :], den[:, :]), m)
        yield
        m = q.op("dve", lambda e: e.tensor_tensor(sc[:, :, :], sc[:, :, :], bc(den[:, :]), ALU.mult), m)
        yield
        chosen, m = yield from router_ranks(q, sb, f"{name}_e", sc, [NT, R], TOPK, m)
    m = q.op("dve", lambda e: e.tensor_tensor(sc[:, :, :], sc[:, :, :], chosen[:, :, :], ALU.mult), m)
    yield
    m = q.op("dve", lambda e: e.tensor_reduce(den[:, :], sc[:, :, :], AX.X, ALU.add), m)
    yield
    if bias is not None:
        m = q.op("dve", lambda e: e.tensor_scalar(den[:, :], den[:, :], 1e-20, None, ALU.add), m)
        yield
    m = q.op("dve", lambda e: e.reciprocal(den[:, :], den[:, :]), m)
    yield
    if FACTOR != 1.0:
        m = q.op("dve", lambda e: e.tensor_scalar(den[:, :], den[:, :], FACTOR, None, ALU.mult), m)
        yield
    m = q.op("dve", lambda e: e.tensor_tensor(
        comb[:, :, shared - 1:shared - 1 + R], sc[:, :, :],
        den[:, :].rearrange("p (t a) -> p t a", a=1).broadcast_to([P, NT, R]), ALU.mult), m)
    yield
    if shared > 1:
        q.op("dve", lambda e: e.memset(comb[:, :, 0:shared - 1], 1.0))


def linear_attention(k, t):
    q, bank, X, YH, YL = k["q"], k["bank"], k["X"], k["YH"], k["YL"]
    ident = k["ident"]
    HN, HD, FD = 16, 32, 64
    G = P // HD
    VA = HD + 1
    NP_ = HN // 2
    s = ExitStack()
    sb = lambda nm, shape, dt=F32: k["sb"](f"lin_{nm}", shape, dt, s)
    raw = sb("raw", [KD, D])
    W1, W2 = ((sb(f"W{i}H", [KD, D], F32R), sb(f"W{i}L", [KD, D], F32R)) for i in (1, 2))
    W = {"k": W1, "v": W2, "q": W1, "o": W2}
    FR = [sb(f"FR{i}", [G * FD]) for i in range(2)]
    F = {w: (sb(f"F{w}H", [G * FD], F32R), sb(f"F{w}L", [G * FD], F32R)) for w in "qk"}
    bq, bk, bv, bo = sb("bq", [KD]), sb("bk", [KD]), sb("bv", [D]), sb("bo", [D])
    am = sb("am", [CT])
    craw = sb("craw", [KD, 512])
    CH, CL = sb("CH", [KD, SC], F32R), sb("CL", [KD, SC], F32R)
    KH, KL = sb("KH", [KD, T], F32R), sb("KL", [KD, T], F32R)
    kf = sb("kf", [HN * FD])
    kfH, kfL = ([sb(f"kf{x}{i}", [HN * FD], F32R) for i in range(2)] for x in "HL")
    v = sb("v", [HN, VA])
    vHL = [sb(f"vHL{i}", [2, HN, VA], F32R) for i in range(2)]
    acc, zero = sb("acc", [B * NP_, 2, 2 * VA]), sb("zero", [D])
    zerob = sb("zerob", [3 * 4 * VA], BF16)
    pairs = {5: (0, 1, 2), 6: (3, 4, 5), 7: (6, 7)}
    kvH, kvL = sb("kvH", [B * NP_, 2 * VA], F32R), sb("kvL", [B * NP_, 2 * VA], F32R)
    qfH, qfL = (c[:, :, :].rearrange("p k (a t) -> p (k a) t", t=T) for c in (CH, CL))
    den = sb("den", [2, HN])
    o = [kf[:, i * D:(i + 1) * D] for i in range(2)]
    oH, oL = ([x[0][:, i * D:(i + 1) * D].rearrange("p (c t) -> p c t", c=KD) for i in range(2)] for x in (kfH, kfL))
    f = NormBuffers(k, s, "lin_n", NT, [kf[:, i * D:(i + 1) * D] for i in range(2)] + [bo[:, :], zero[:, :]])

    def load_weights(x):
        return q.load("w", lambda e: e.dma_start(
            raw[:, :, :], t[f"l_{x}"].rearrange("(k p) n -> p k n", p=P)), *q.at("raw read"))

    def split_weights(x, loaded, *free, engines=("dve", "pool")):
        ms = [split(q, engines[kk % 2], W[x][0][:, kk, :], W[x][1][:, kk, :], raw[:, kk, :], loaded, *free)
              for kk in range(KD)]
        q.note("raw read", *ms[-2:])
        return ms[-2:]

    w = lambda x, kk, a: (W[x][0][:, kk, a], W[x][1][:, kk, a])
    wk_in = load_weights("k")
    q.load("small", lambda e: e.dma_start(bq[:, :], t["l_bq"]))
    q.load("small", lambda e: e.dma_start(bk[:, :], t["l_bk"]))
    everywhere = lambda sem, to, of, *waits: q.load(sem, lambda e: e.dma_start(
        to[:, :], t[of].rearrange("(a n) -> a n", a=1).broadcast_to([P, D])), *waits)
    small = everywhere("small", bv, "l_bv")
    fr = {}
    for i, x in enumerate("kq"):
        m = q.op("pool", lambda e: e.memset(FR[i][:, :], 0.0))
        for g in range(G):
            fr[x] = q.load(("w2", "turn0")[i], lambda e: e.dma_start(
                FR[i][g * HD:(g + 1) * HD, g * FD:(g + 1) * FD], t[f"l_{x}f"]), m)
    q.op("pool", lambda e: e.memset(v[:, :, HD:VA], 1.0))
    z = q.op("pool", lambda e: e.memset(zerob[:, :], 0.0))
    for kv in (kvH, kvL):
        kvz = q.op("pool", lambda e: e.memset(kv[:, :, :].bitcast(F32), 0.0))
    for i, x in enumerate("kq"):
        fs = split(q, "pool", F[x][0][:, :], F[x][1][:, :], FR[i][:, :], fr[x])
    for e_ in ("act", "dve", "pe", "pool"):
        q.wait(e_, small, z, kvz, fs)
    wk = split_weights("k", wk_in)
    wv_in = load_weights("v")
    norm(k, f, NT, lambda i: X[:, i, :], YH, YL)
    q.note("kf read", *q.at("y"))
    q.wait("dve", q.op("dve", lambda e: e.memset(zero[:, :], 0.0), *q.at("y")))
    wv = split_weights("v", wv_in, engines=("dve", "dve"))

    def keys_values(b):
        vm, fm, km = {}, {}, {}

        def context(h):
            hs = slice(h * 512, h * 512 + 512)
            m = q.load("ctx", lambda e: e.dma_start(craw[:, :, :], t["ctxT"][b, :, :, hs]), *q.at("craw read"))
            ms = []
            for kk in range(KD):
                cm = split(q, ("dve", "pool")[kk % 2], CH[:, kk, hs], CL[:, kk, hs], craw[:, kk, :], m, *q.at(f"C{h} read"))
                ms.append(cm)
            q.note("craw read", *ms[-2:])
            return ms[-2:]

        def keys(h):
            hs = slice(h * 512, h * 512 + 512)
            for c in range(KD):
                m = product(q, bank[c][:, :], [w("k", kk, slice(c * P, c * P + P)) for kk in range(KD)],
                            [(CH[:, kk, hs], CL[:, kk, hs]) for kk in range(KD)], *wk, *cm[h],
                            *q.at(f"bank{c} read"))
                km[c] = split(q, "dve", KH[:, c, :], KL[:, c, :], bank[c][:, :], m, *q.at("K read"),
                              bias=bk[:, c:c + 1])
                q.note(f"bank{c} read", km[c])
            q.note("W1 read", m)

        def values_and_features(i):
            a = slice(i * P, i * P + P)
            ka = slice(i % 4 * P, i % 4 * P + P)
            r = 4
            m = product(q, bank[r][:, :], [(CH[:, kk, a], CL[:, kk, a]) for kk in range(KD)],
                        [w("v", kk, slice(0, D)) for kk in range(KD)], *wv, *cm[i // 4], *q.at(f"bank{r} read"))
            if i % 4 == 3:
                q.note(f"C{i // 4} read", m)
            q.note("W2 read", m)
            added = q.op("dve", lambda e: e.tensor_tensor(
                v[:, :, 0:HD], bank[r][:, :].rearrange("p (h e) -> p h e", e=HD),
                bv[:, :].rearrange("p (h e) -> p h e", e=HD), ALU.add), m, *q.at("v read"))
            q.note(f"bank{r} read", added)
            kfm = []
            for c in range(2):
                r = (2 * i + c) % 4
                for d in range(2):
                    m = product(q, bank[r][:, d * 256:(d + 1) * 256],
                                [(KH[:, 2 * c + d, ka], KL[:, 2 * c + d, ka])],
                                [(F["k"][0][:, :], F["k"][1][:, :])], km[2 * c + d], *q.at(f"bank{r} read"))
                fs = slice(c * 512, c * 512 + 512)
                kfm.append(q.op("dve", lambda e: e.tensor_scalar(
                    kf[:, fs], bank[r][:, :], 0.0, am[:, i:i + 1], ALU.max, ALU.mult), m, small,
                    *q.at("kf read")))
                q.note(f"bank{r} read", kfm[-1])
            q.note("K read", m)
            vm[i] = split(q, "dve", vHL[i % 2][:, 0, :, :], vHL[i % 2][:, 1, :, :], v[:, :, :], added,
                          *q.at(f"kv{i % 2} read"))
            q.note("v read", vm[i])
            for c in range(2):
                fs = slice(c * 512, c * 512 + 512)
                fm[i] = split(q, "dve", kfH[i % 2][:, fs], kfL[i % 2][:, fs], kf[:, fs], kfm[c],
                              *q.at(f"kv{i % 2} read"))
            q.note("kf read", fm[i])

        def contract(i):
            for r, ps in pairs.items():
                n = len(ps) * 4 * VA
                nothing = lambda e, at: e.matmul(bank[r][:, 0:n], k["identb"][:, :], zerob[:, 0:n],
                                                 start=at == "start", stop=at == "stop")
                if i == 0:
                    q.quiet("pe", lambda e: nothing(e, "start"), *q.at(f"bank{r} read"))
                for d, p_ in enumerate(ps):
                    fs = slice(p_ * P, p_ * P + P)
                    at = d * 4 * VA
                    both = vHL[i % 2][:, :, 2 * p_:2 * p_ + 2, :].rearrange("p x h e -> p x (h e)")
                    q.quiet("pe", lambda e: e.matmul(
                        bank[r][:, at:at + 4 * VA], kfH[i % 2][:, fs], both, start=False, stop=False,
                        skip_group_check=True), fm[i], vm[i])
                    m = q.op("pe", lambda e: e.matmul(
                        bank[r][:, at:at + 2 * VA], kfL[i % 2][:, fs], both[:, 0, :], start=False, stop=False,
                        skip_group_check=True))
                if i == CT - 1:
                    m = q.op("pe", lambda e: nothing(e, "stop"))
                    m2 = q.op("dve", lambda e: e.tensor_tensor(
                        acc[:, bass.ds(b * NP_ + ps[0], len(ps)), :, :].rearrange("p a x e -> p (a x e)"),
                        bank[r][:, 0:n], zero[:, 0:n], ALU.add), m)
                    q.note(f"bank{r} read", m2)
                    q.note("acc", m2)
            q.note(f"kv{i % 2} read", m)

        cm = {0: context(0)}
        small = q.load("small", lambda e: e.dma_start(am[:, :], t["l_mask"][b]), *q.at("am read"))
        for i in range(CT):
            if i == 2:
                cm[1] = context(1)
            if i % 4 == 0:
                keys(i // 4)
            values_and_features(i)
            if i >= 1:
                contract(i - 1)
        contract(CT - 1)
        q.note("am read", *q.at("kf read"))

    q.loop(B, keys_values)
    wq_in = load_weights("q")
    bo_in = everywhere("turn1", bo, "l_bo", *q.at("y"))
    wq = split_weights("q", wq_in, *q.at("W1 read"))
    wo = split_weights("o", load_weights("o"), *q.at("W2 read"))
    last = q.at("K read") + q.at("kv0 read") + q.at("kv1 read")
    both = q.op("dve", lambda e: e.tensor_tensor(acc[:, :, 0, :], acc[:, :, 0, :], acc[:, :, 1, :], ALU.add),
                *q.at("acc"))
    for h in range(2):
        ps, es = slice(h * FD, (h + 1) * FD), slice(h * VA, (h + 1) * VA)
        kvm = split(q, "dve", kvH[ps, :, es], kvL[ps, :, es], acc[ps, :, 0, es], both)
    ym = q.at("y")
    for e_ in ("act", "dve", "pe"):
        q.wait(e_, *last)
    q.wait("dve", bo_in)

    def queries(b):
        QH, QL = KH, KL
        qm, pm, num, tr = {}, {}, {}, {}

        def query(c):
            r = c % 2
            m = product(q, bank[r][:, :], [w("q", kk, slice(c * P, c * P + P)) for kk in range(KD)],
                        [(YH[:, kk, bass.ds(b * T, T)], YL[:, kk, bass.ds(b * T, T)]) for kk in range(KD)],
                        *wq, *ym, *q.at(f"bank{r} read"))
            qm[c] = split(q, "dve", QH[:, c, :], QL[:, c, :], bank[r][:, :], m, *q.at("Q read"),
                          bias=bq[:, c:c + 1])
            q.note(f"bank{r} read", qm[c])

        def features(c):
            for d in range(2):
                p_ = 2 * c + d
                r = 2 + p_ % 2
                m = product(q, bank[r][:, :], [(F["q"][0][:, d * P:(d + 1) * P], F["q"][1][:, d * P:(d + 1) * P])],
                            [(QH[:, c, :], QL[:, c, :])], qm[c], *q.at(f"bank{r} read"))
                hi = q.op("act", lambda e: e.activation(qfH[:, p_, :], bank[r][:, :], ACT.Relu), m,
                          *q.at("qf read"))
                pm[p_] = q.op("dve", lambda e: e.scalar_tensor_tensor(
                    out=qfL[:, p_, :], in0=bank[r][:, :], scalar=0.0, in1=qfH[:, p_, :].bitcast(F32),
                    op0=ALU.max, op1=ALU.subtract), hi)
                q.note(f"bank{r} read", pm[p_])
            if c == KD - 1:
                q.note("Q read", m)

        def readout(i):
            a = slice(i * P, i * P + P)
            for c in range(2):
                r = (4, 5, 6, 7)[(2 * i + c) % 4]
                for d in range(4):
                    p_ = 4 * c + d
                    m = product(q, bank[r][:, d * 2 * VA:(d + 1) * 2 * VA], [(qfH[:, p_, a], qfL[:, p_, a])],
                                [tuple(x[:, bass.ds(b * NP_ + p_, 1), :].rearrange("p a e -> p (a e)")
                                       for x in (kvH, kvL))], pm[p_], kvm, *q.at(f"bank{r} read"))
                hs = slice(8 * c, 8 * c + 8)
                nu = bank[r][:, 0:8 * VA].rearrange("p (h e) -> p h e", e=VA)
                dh = den[:, i % 2, hs]
                m1 = q.op("dve", lambda e: e.tensor_scalar(dh, nu[:, :, HD], 1e-8, None, ALU.add), m)
                m1 = q.op("dve", lambda e: e.reciprocal(dh, dh), m1)
                num[i] = q.op("dve", lambda e: e.tensor_tensor(
                    o[i % 2][:, 8 * c * HD:8 * (c + 1) * HD].rearrange("p (h e) -> p h e", e=HD), nu[:, :, 0:HD],
                    dh.rearrange("p (h a) -> p h a", a=1).broadcast_to([P, 8, HD]), ALU.mult), m1,
                    *q.at(f"o{i % 2} read"))
                q.note(f"bank{r} read", num[i])
            if i == TT - 1:
                q.note("qf read", m)

        def transposed(i):
            r = i % 2
            for c in range(KD):
                m = q.op("pe", lambda e: e.transpose(bank[r][:, c * P:(c + 1) * P], o[i % 2][:, c * P:(c + 1) * P],
                                                     ident[:, :]), num[i], *q.at(f"bank{r} read"))
            q.note(f"o{i % 2} read", m)
            tr[i] = split(q, "dve", oH[i % 2], oL[i % 2], bank[r][:, :].rearrange("p (c t) -> p c t", c=KD), m,
                          *q.at(f"oH{i % 2} read"))
            q.note(f"bank{r} read", tr[i])

        def project(i):
            r = 2 + i % 2
            m = product(q, bank[r][:, :], [(oH[i % 2][:, c, :], oL[i % 2][:, c, :]) for c in range(KD)],
                        [w("o", c, slice(0, D)) for c in range(KD)], tr[i], *wo, *q.at(f"bank{r} read"))
            q.note(f"oH{i % 2} read", m)
            xs = X[:, bass.ds(b * TT + i, 1), :].rearrange("p a d -> p (a d)")
            x1 = q.op("dve", lambda e: e.tensor_tensor(xs, bank[r][:, :], xs, ALU.add), m)
            q.note(f"bank{r} read", x1)
            q.note("x", q.op("dve", lambda e: e.tensor_tensor(xs, xs, bo[:, :], ALU.add), x1))

        for c in range(KD + 1):
            if c < KD:
                query(c)
            if c >= 1:
                features(c - 1)
        for i in range(TT + 2):
            if i < TT:
                readout(i)
            if 1 <= i <= TT:
                transposed(i - 1)
            if i >= 2:
                project(i - 2)

    q.loop(B, queries)
    q.fence()
    s.close()


_OUT = [((B, T, D), "float32")]


def _laid_out(i):
    import numpy as np

    c = np.ascontiguousarray

    def by_rows(w):
        return w.reshape(KD, P, -1).transpose(1, 0, 2)

    def qkv(wq, wk, wv):
        return c(np.stack([np.concatenate([by_rows(x) for x in parts], axis=2) for parts in zip(wq, wk, wv)]))

    a = {}
    a["x"] = i["x"]
    ctx = i["ctx_2048"]
    a["ctxT"] = c(ctx.transpose(0, 2, 1).reshape(B, KD, P, SC).transpose(0, 2, 1, 3))
    a["ctx"] = c(ctx.reshape(B, CT, P, D).transpose(0, 2, 1, 3))
    a["mem_mask"] = i["mask_BxS2_bk0"]
    cut = [slice(j * P, j * P + P) for j in range(4)]
    q, kk, v, o = (i[f"L0_attn_W{x}"].T for x in "qkvo")
    a["a0_qkv"] = qkv([q[:, s] for s in cut], [kk[:, s] for s in cut], [v[:, s] for s in cut])
    a["a0_wo"] = c(np.stack([o[s][:, None] for s in cut]))
    w = i["L1_attn_w_in"].T
    q = w[:, :2048].reshape(D, 4, 2, 4, 64).transpose(1, 0, 3, 2, 4).reshape(4, D, 512)
    kk, v = w[:, 2048:2560], w[:, 2560:]
    a["a1_qkv"] = qkv(list(q), [kk[:, s] for s in cut], [v[:, s] for s in cut])
    o = i["L1_attn_w_out"].T.reshape(4, 2, 4, 64, D).transpose(0, 1, 3, 2, 4)
    a["a1_wo"] = c(o.reshape(4, P, 4, D))
    a["rms_w"] = i["L1_attn_rms_w"].reshape(KD, P).T
    freq = 1.0 / np.float32(10000.0) ** (np.arange(0, 64, 2, dtype=np.float32) / np.float32(64))
    ang = np.arange(T, dtype=np.float32)[None, :] * freq[:, None]
    co, si = np.cos(ang), np.sin(ang)
    a["rotary"] = np.stack([np.tile(co, (4, 1)), np.concatenate([-si, si, -si, si])], axis=1)
    two = lambda x: [x[:INNER], x[INNER:]]
    gate = np.stack(two(i["L0_ffn_shared_gate_w"]) + list(i["L0_ffn_gate_proj"]))
    up = np.stack(two(i["L0_ffn_shared_up_w"]) + list(i["L0_ffn_up_proj"]))
    gu = np.concatenate([gate, up], axis=1).transpose(0, 2, 1)
    a["f0_up"] = c(gu.reshape(18, KD, P, 2 * INNER).transpose(0, 2, 1, 3))
    down = np.stack(two(i["L0_ffn_shared_down_w"].T) + [x.T for x in i["L0_ffn_down_proj"]])
    a["f0_down"] = c(down)
    a["f0_router"] = c(i["L0_ffn_gate_weight"].T)
    a["f0_bias"] = i["L0_ffn_e_score_correction_bias"]
    w1 = np.stack([i["L1_ffn_w_shared1"]] + list(i["L1_ffn_w1"]))
    a["f1_up"] = c(w1.reshape(9, KD, P, INNER).transpose(0, 2, 1, 3))
    a["f1_down"] = c(np.stack([i["L1_ffn_w_shared2"]] + list(i["L1_ffn_w2"])))
    a["f1_router"] = i["L1_ffn_w_router"]
    for x in "qkvo":
        a[f"l_{x}"] = c(i[f"L1_xattn_W{x}"].T)
        a[f"l_b{x}"] = i[f"L1_xattn_b{x}"]
    for x in "qk":
        a[f"l_{x}f"] = c(i[f"L1_xattn_W{x}f"].T)
    for x in "qk":
        a[f"l_b{x}"] = a[f"l_b{x}"].reshape(KD, P).T
    a["l_mask"] = i["mask_BxS2_ff1"].reshape(B, CT, P).transpose(0, 2, 1)
    return {n: c(x) for n, x in a.items()}


def kernel(**inputs):
    import numpy as np
    import concourse.bacc as bacc
    from concourse.bass_utils import run_bass_kernel_spmd

    nc = bacc.Bacc("TRN2", target_bir_lowering=False, num_devices=1)
    arrays = _laid_out({n: np.asarray(x) for n, x in inputs.items()})
    t = {n: nc.dram_tensor(n, x.shape, mybir.dt.from_np(x.dtype), kind="ExternalInput").ap()
         for n, x in arrays.items()}
    t["out"] = nc.dram_tensor("out", _OUT[0][0], F32, kind="ExternalOutput").ap()
    program(nc, t)
    r = run_bass_kernel_spmd(nc, [arrays], core_ids=[0])
    return r.results[0]["out"]
```
